# Optimizing a Trainium2 kernel written in Bass

```python
import numpy as np
import jax
import jax.numpy as jnp

def _softmax(x, axis=-1):
    return jax.nn.softmax(x, axis=axis)

def _gelu(x):
    return jax.nn.gelu(x, approximate=True)

def _silu(x):
    return jax.nn.silu(x)

def _sigmoid(x):
    return jax.nn.sigmoid(x)

def _layernorm(x, axis=-1, eps=1e-05):
    m = jnp.mean(x, axis=axis, keepdims=True)
    v = jnp.var(x, axis=axis, keepdims=True)
    return (x - m) / jnp.sqrt(v + eps)

def _scatter_add(tgt, idx, src, axis=0):
    return tgt.at[idx].add(src)

def _segment_sum(src, seg, n):
    return jax.ops.segment_sum(src, seg, n)
kernel_name = 'mk_adaln_ffn_d2_seqx_r2_715063'

def setup_inputs(seed: int=0):
    np.random.seed(seed)
    _w = jnp.asarray

    def _rec_inputs():
        import jax
        import jax.numpy as jnp
        _rk = jax.random.key(seed)
        x = -0.000125 + 0.9999 * jax.random.normal(jax.random.fold_in(_rk, 1), (32, 128, 2048), jnp.float32)
        _lenS = 128 - jax.random.randint(jax.random.fold_in(_rk, 7), (32,), 0, max(1, 128 // 4) + 1, jnp.int32)
        _lenS2 = 128 - jax.random.randint(jax.random.fold_in(_rk, 8), (32,), 0, max(1, 128 // 4) + 1, jnp.int32)
        cond_128 = 0.0061147 + 1.02565 * jax.random.normal(jax.random.fold_in(_rk, 11), (32, 128), jnp.float32)
        fside_S_0 = -0.022604 + 0.987366 * jax.random.normal(jax.random.fold_in(_rk, 12), (128,), jnp.float32)
        return (x, cond_128, fside_S_0)
    x, cond_128, fside_S_0 = _rec_inputs()

    def _L0_cond_setup():
        import jax, jax.numpy as jnp
        import numpy as np
        K = 8
        T = 1.0
        D_EMBD = 128
        IN_C = 128
        OUT_C = 128
        BS = 32
        H = 2048
        HID = 128
        key = jax.random.key(seed)
        ks = jax.random.split(key, 10)
        s = lambda fan_in: 1.0 / np.sqrt(fan_in)
        return {'x': jax.random.normal(ks[0], (BS, IN_C, H), dtype=jnp.float32), 'embedding': jax.random.normal(ks[1], (BS, D_EMBD), dtype=jnp.float32), 'W0': jax.random.normal(ks[2], (D_EMBD, HID), dtype=jnp.float32) * s(D_EMBD), 'b0': jnp.zeros((HID,), dtype=jnp.float32), 'W1': jax.random.normal(ks[3], (HID, HID), dtype=jnp.float32) * s(HID), 'b1': jnp.zeros((HID,), dtype=jnp.float32), 'W2': jax.random.normal(ks[4], (HID, K), dtype=jnp.float32) * s(HID), 'b2': jnp.zeros((K,), dtype=jnp.float32), 'weight': jax.random.normal(ks[5], (K, OUT_C, IN_C, 1), dtype=jnp.float32) * s(IN_C), 'bias_k': jax.random.normal(ks[6], (K, OUT_C), dtype=jnp.float32) * 0.1}
    _L0_cond_all = _L0_cond_setup()
    _L0_cond_in = {k: v for k, v in _L0_cond_all.items() if k in ('W0', 'b0', 'W1', 'b1', 'W2', 'b2', 'weight', 'bias_k')}
    del _L0_cond_all

    def _L0_ffn_setup():
        import jax, jax.numpy as jnp
        import numpy as np
        key = jax.random.key(seed)
        k = jax.random.split(key, 6)
        x = jax.random.normal(k[0], (4, 1024, 2048), jnp.float32)
        W = jax.random.normal(k[1], (2048, 2048), jnp.float32) * 0.02
        bias = jax.random.normal(k[2], (2048,), jnp.float32) * 0.02
        A = jax.random.normal(k[3], (16, 16, 2048), jnp.float32) * 0.02
        Bf = jax.random.normal(k[4], (16, 2048, 16), jnp.float32) * 0.02
        coeffs = jax.random.uniform(k[5], (16,), jnp.float32)
        scales = jnp.full((16,), 0.5, jnp.float32)
        return {'x': x, 'W': W, 'bias': bias, 'A': A, 'Bf': Bf, 'coeffs': coeffs, 'scales': scales}
    _L0_ffn_all = _L0_ffn_setup()
    _L0_ffn_in = {k: v for k, v in _L0_ffn_all.items() if k in ('W', 'bias', 'A', 'Bf', 'coeffs', 'scales')}
    del _L0_ffn_all

    def _L1_cond_setup():
        import jax, jax.numpy as jnp
        import numpy as np
        from jax import lax
        N, C_IN, L = (32, 128, 2048)
        C_OUT, K, GROUPS = (128, 9, 4)
        C_DIM, PAD, STRIDE = (128, 4, 1)
        key = jax.random.key(seed)
        k1, k2, k3, k4, k5 = jax.random.split(key, 5)
        x = jax.random.normal(k1, (N, C_IN, L), dtype=jnp.float32)
        c = jax.random.normal(k2, (N, C_DIM), dtype=jnp.float32)
        weight = jax.random.normal(k3, (C_OUT, C_IN // GROUPS, K), dtype=jnp.float32)
        c_weight = jax.random.normal(k4, (C_OUT, C_DIM), dtype=jnp.float32)
        bias = jax.random.normal(k5, (C_OUT,), dtype=jnp.float32)
        return {'x': x, 'c': c, 'weight': weight, 'c_weight': c_weight, 'bias': bias}
    _L1_cond_all = _L1_cond_setup()
    _L1_cond_in = {k: v for k, v in _L1_cond_all.items() if k in ('weight', 'c_weight')}
    del _L1_cond_all

    def _L1_ffn_setup():
        import jax, jax.numpy as jnp
        import numpy as np
        B, L, H, Dh, M = (4, 1024, 16, 128, 512)
        D = H * Dh
        key = jax.random.key(seed)
        kx, ku, kd, kp = jax.random.split(key, 4)
        x = jax.random.normal(kx, (B, L, D), dtype=jnp.float32)
        up = jax.random.normal(ku, (H, Dh, M), dtype=jnp.float32)
        down = jax.random.normal(kd, (H, M, Dh), dtype=jnp.float32)
        perm = jax.random.permutation(kp, D)
        return {'x': x, 'up': up, 'down': down, 'perm': perm}
    _L1_ffn_all = _L1_ffn_setup()
    _L1_ffn_in = {k: v for k, v in _L1_ffn_all.items() if k in ('up', 'down', 'perm')}
    del _L1_ffn_all
    return {'x': x, 'cond_128': cond_128, 'fside_S_0': fside_S_0, 'L0_cond_W0': _L0_cond_in['W0'], 'L0_cond_b0': _L0_cond_in['b0'], 'L0_cond_W1': _L0_cond_in['W1'], 'L0_cond_b1': _L0_cond_in['b1'], 'L0_cond_W2': _L0_cond_in['W2'], 'L0_cond_b2': _L0_cond_in['b2'], 'L0_cond_weight': _L0_cond_in['weight'], 'L0_cond_bias_k': _L0_cond_in['bias_k'], 'L0_ffn_W': _L0_ffn_in['W'], 'L0_ffn_bias': _L0_ffn_in['bias'], 'L0_ffn_A': _L0_ffn_in['A'], 'L0_ffn_Bf': _L0_ffn_in['Bf'], 'L0_ffn_coeffs': _L0_ffn_in['coeffs'], 'L0_ffn_scales': _L0_ffn_in['scales'], 'L1_cond_weight': _L1_cond_in['weight'], 'L1_cond_c_weight': _L1_cond_in['c_weight'], 'L1_ffn_up': _L1_ffn_in['up'], 'L1_ffn_down': _L1_ffn_in['down'], 'L1_ffn_perm': _L1_ffn_in['perm']}

def reference(x, cond_128, fside_S_0, L0_cond_W0, L0_cond_b0, L0_cond_W1, L0_cond_b1, L0_cond_W2, L0_cond_b2, L0_cond_weight, L0_cond_bias_k, L0_ffn_W, L0_ffn_bias, L0_ffn_A, L0_ffn_Bf, L0_ffn_coeffs, L0_ffn_scales, L1_cond_weight, L1_cond_c_weight, L1_ffn_up, L1_ffn_down, L1_ffn_perm):
    import jax
    import jax.numpy as jnp

    def _L0_cond_ref(x, embedding, W0, b0, W1, b1, W2, b2, weight, bias_k):
        import jax, jax.numpy as jnp
        import numpy as np
        K = 8
        T = 1.0
        D_EMBD = 128
        IN_C = 128
        OUT_C = 128
        BS = 32
        H = 2048
        HID = 128
        h = jax.nn.gelu(embedding @ W0 + b0, approximate=False)
        h = jax.nn.gelu(h @ W1 + b1, approximate=False)
        att = jax.nn.softmax((h @ W2 + b2) / T, axis=-1)
        agg_w = jnp.einsum('bk,koi->boi', att, weight[..., 0])
        agg_b = att @ bias_k
        out = jnp.einsum('boi,bih->boh', agg_w, x) + agg_b[:, :, None]
        return out

    def _L0_ffn_ref(x, W, bias, A, Bf, coeffs, scales):
        import jax, jax.numpy as jnp
        import numpy as np
        out = jnp.einsum('bsd,od->bso', x, W) + bias
        xa = jnp.einsum('bsd,erd->ebsr', x, A)
        w = coeffs * scales
        upd = jnp.einsum('ebsr,eor,e->bso', xa, Bf, w)
        return out + upd

    def _L1_cond_ref(x, c, weight, c_weight, bias):
        import jax, jax.numpy as jnp
        import numpy as np
        from jax import lax
        N, C_IN, L = (32, 128, 2048)
        C_OUT, K, GROUPS = (128, 9, 4)
        C_DIM, PAD, STRIDE = (128, 4, 1)
        out = lax.conv_general_dilated(x, weight, window_strides=(STRIDE,), padding=[(PAD, PAD)], dimension_numbers=('NCH', 'OIH', 'NCH'), feature_group_count=GROUPS)
        ctx = jnp.einsum('nd,od->no', c, c_weight)
        out = out + ctx[:, :, None] + bias[None, :, None]
        return out

    def _L1_ffn_ref(x, up, down, perm):
        import jax, jax.numpy as jnp
        import numpy as np
        B, L, H, Dh, M = (4, 1024, 16, 128, 512)
        D = H * Dh
        b, l, Dm = x.shape
        h, d = (up.shape[0], up.shape[1])
        unperm = jnp.argsort(perm)
        t = x.reshape(b * l, Dm)
        t = t[:, perm]
        t = t.reshape(b * l, h, d)
        t = jnp.einsum('bhd,hdm->bhm', t, up)
        t = jax.nn.gelu(t, approximate=False)
        t = jnp.einsum('bhm,hmd->bhd', t, down)
        t = t.reshape(b * l, h * d)
        t = t[:, unperm]
        out = t.reshape(b, l, Dm)
        return out
    x = x + _L0_ffn_ref(_L0_cond_ref(x, cond_128, L0_cond_W0, L0_cond_b0, L0_cond_W1, L0_cond_b1, L0_cond_W2, L0_cond_b2, L0_cond_weight, L0_cond_bias_k), L0_ffn_W, L0_ffn_bias, L0_ffn_A, L0_ffn_Bf, L0_ffn_coeffs, L0_ffn_scales)
    x = x + _L1_ffn_ref(_L1_cond_ref(x, cond_128, L1_cond_weight, L1_cond_c_weight, fside_S_0), L1_ffn_up, L1_ffn_down, L1_ffn_perm)
    return x

_drawn_inputs = setup_inputs


def setup_inputs(seed=0):
    import zlib

    import numpy as np

    out = dict(_drawn_inputs(seed))
    spreads = {'L0_cond_b0': (0.0, 0.657),
     'L0_cond_b1': (0.0, 0.412),
     'L0_cond_b2': (0.0, 0.372),
     'L0_ffn_scales': (0.5, 0.6)}
    factors = {'L0_ffn_bias': 3.416, 'L0_ffn_coeffs': 5.354}
    for name, (base, spread) in spreads.items():
        noise = np.random.default_rng([zlib.crc32(name.encode()), seed]).standard_normal(out[name].shape)
        drawn = base * np.exp(spread * noise) if base else spread * noise
        out[name] = jnp.asarray(drawn.astype(out[name].dtype))
    for name, factor in factors.items():
        out[name] = (out[name] * factor).astype(out[name].dtype)
    return out
```

```python
import concourse.bass as bass
from concourse import mybir
from contextlib import ExitStack

F32 = mybir.dt.float32
F32R = mybir.dt.float32r
I32 = mybir.dt.int32
ALU = mybir.AluOpType
ACT = mybir.ActivationFunctionType
AX = mybir.AxisListType

P = 128
NB, C, L = 32, 128, 2048
DC = L // P
HALF = L // 2
K = 8
ER = 256
KC = ER // P
G, GC, TAPS, S = 4, 32, 9, 4
Q = L // S
H, M = 16, 512
MC = M // P
RB = 512
BLOCKS = NB * C // RB
SB = RB // C
LEAD = 20


def wait(eng, sem, value):
    if isinstance(value, int) and value <= 0:
        return
    eng.wait_ge(sem, value)


def fp32(ap):
    return ap.bitcast(F32)


def setup_block(nc, cond_t, w0, b0, w1, b1, w2, b2, w_t, lora_a, lora_b, coeffs, scales, att_d, weff_d):
    with ExitStack() as ctx:
        def sb(name, shape, dt=F32):
            return ctx.enter_context(nc.sbuf_tensor(name, shape, dt))

        def sem(name):
            return ctx.enter_context(nc.semaphore(name))

        cond_s = sb("cond_s", [P, NB])
        w0_s, w1_s, w2_s = sb("w0_s", [P, P]), sb("w1_s", [P, P]), sb("w2_s", [P, K])
        b0_s, b1_s, b2_s = sb("b0_s", [P, 1]), sb("b1_s", [P, 1]), sb("b2_s", [NB, K])
        h0, h1 = sb("h0", [P, NB]), sb("h1", [P, NB])
        logits, expo, att = sb("logits", [NB, K]), sb("expo", [NB, K]), sb("att", [NB, K])
        peak, total, inverse = sb("peak", [NB, 1]), sb("total", [NB, 1]), sb("inverse", [NB, 1])
        co_s, sc_s, cs = sb("co_s", [P, KC]), sb("sc_s", [P, KC]), sb("cs", [P, KC])
        b_in_s, b_sc = sb("b_in_s", [P, KC, L]), sb("b_sc", [P, KC, L])
        b_hi, b_lo = sb("b_hi", [P, KC, L], F32R), sb("b_lo", [P, KC, L], F32R)
        a_s = [sb(f"a_s{j}", [P, KC, P]) for j in range(2)]
        a_hi = [sb(f"a_hi{j}", [P, KC, P], F32R) for j in range(2)]
        a_lo = [sb(f"a_lo{j}", [P, KC, P], F32R) for j in range(2)]
        wt_s = [sb(f"wt_s{j}", [P, L]) for j in range(2)]
        we_s = [sb(f"we_s{j}", [P, L]) for j in range(2)]
        acc = ctx.enter_context(nc.psum_tensor("acc", [P, 2, 4, 512], F32))
        ps_h0, ps_h1, ps_lg = acc[:, 1, 0, 0:NB], acc[:, 1, 1, 0:NB], acc[0:NB, 1, 2, 0:K]

        cond_in, lora_in = sem("cond_in"), sem("lora_in")
        aw_in = [sem(f"aw_in{j}") for j in range(2)]
        h0_mm, h0_ready, h1_mm, h1_ready = sem("h0_mm"), sem("h0_ready"), sem("h1_mm"), sem("h1_ready")
        lg_mm, lg_ready, peak_ready, exp_ready, att_ready = (sem(n) for n in (
            "lg_mm", "lg_ready", "peak_ready", "exp_ready", "att_ready"))
        sm_step, att_out = sem("sm_step"), sem("att_out")
        cs_ready, bsc_ready, bhi_ready, blo_ready = sem("cs_ready"), sem("bsc_ready"), sem("bhi_ready"), sem("blo_ready")
        ahi_ready, alo_ready, weff_mm, weff_ready = sem("ahi_ready"), sem("alo_ready"), sem("weff_mm"), sem("weff_ready")
        weff_out = [sem(f"weff_out{j}") for j in range(2)]
        block = ctx.enter_context(nc.Block())

        a_v = lora_a.rearrange("(c p) d -> p c d", p=P)
        b_v = lora_b.rearrange("(c p) n -> p c n", p=P)

        @block.sync
        def _(sp):
            for dst, src in ((cond_s, cond_t), (w0_s, w0), (w1_s, w1), (w2_s, w2),
                             (b0_s, b0.rearrange("(p a) -> p a", a=1)), (b1_s, b1.rearrange("(p a) -> p a", a=1)),
                             (b2_s, b2.rearrange("(a k) -> a k", a=1).to_broadcast([NB, K]))):
                sp.dma_start(dst[:], src).then_inc(cond_in, 16)
            sp.dma_start(co_s[:], coeffs).then_inc(lora_in, 16)
            sp.dma_start(sc_s[:], scales).then_inc(lora_in, 16)
            sp.dma_start(b_in_s[:], b_v).then_inc(lora_in, 16)

            def load(i, j):
                dc = 2 * i + j
                wait(sp, alo_ready, dc - 1)
                wait(sp, weff_ready, dc - 1)
                sp.dma_start(a_s[j][:], a_v[:, :, bass.ds(dc * P, P)]).then_inc(aw_in[j], 16)
                sp.dma_start(wt_s[j][:], w_t[bass.ds(dc * P, P), :]).then_inc(aw_in[j], 16)

            load(0, 0)
            load(0, 1)
            with sp.Fori(1, DC // 2) as i:
                load(i, 0)
                load(i, 1)

        @block.tensor
        def _(pe):
            pe.wait_ge(cond_in, 7 * 16)
            nc.tensor.matmul(ps_h0, w0_s[:], cond_s[:], start=True, stop=True).then_inc(h0_mm, 1)
            pe.wait_ge(h0_ready, 1)
            nc.tensor.matmul(ps_h1, w1_s[:], h0[:], start=True, stop=True).then_inc(h1_mm, 1)
            pe.wait_ge(h1_ready, 1)
            nc.tensor.matmul(ps_lg, h1[:], w2_s[:], start=True, stop=True).then_inc(lg_mm, 1)
            pe.wait_ge(bhi_ready, KC)
            pe.wait_ge(blo_ready, KC)

            def chunk(i, j):
                dc = 2 * i + j
                pe.wait_ge(alo_ready, dc + 1)
                wait(pe, weff_ready, dc - 1)
                if isinstance(dc, int) and dc == 1:
                    pe.wait_ge(lg_ready, 1)
                for kc in range(KC):
                    for w, b in ((a_hi, b_hi), (a_hi, b_lo), (a_lo, b_hi)):
                        for n in range(4):
                            mm = nc.tensor.matmul(acc[:, j, n, :], w[j][:, kc, :], b[:, kc, n * 512:(n + 1) * 512],
                                                  start=(kc == 0 and w is a_hi and b is b_hi),
                                                  stop=(kc == KC - 1 and w is a_lo))
                mm.then_inc(weff_mm, 1)

            chunk(0, 0)
            chunk(0, 1)
            with pe.Fori(1, DC // 2) as i:
                chunk(i, 0)
                chunk(i, 1)

        @block.scalar
        def _(act):
            act.wait_ge(h0_mm, 1)
            nc.scalar.activation(h0[:], ps_h0, ACT.Gelu, bias=b0_s[:]).then_inc(h0_ready, 1)
            act.wait_ge(h1_mm, 1)
            nc.scalar.activation(h1[:], ps_h1, ACT.Gelu, bias=b1_s[:]).then_inc(h1_ready, 1)
            act.wait_ge(peak_ready, 1)
            nc.scalar.activation(expo[:], logits[:], ACT.Exp).then_inc(exp_ready, 1)
            for c in range(KC):
                act.wait_ge(bsc_ready, c + 1)
                nc.scalar.activation(b_hi[:, c, :], b_sc[:, c, :], ACT.Copy).then_inc(bhi_ready, 1)

            def split_a(i, j):
                dc = 2 * i + j
                act.wait_ge(aw_in[j], 32 * i + 32)
                wait(act, weff_mm, dc - 1)
                nc.scalar.activation(a_hi[j][:], a_s[j][:], ACT.Copy).then_inc(ahi_ready, 1)

            def store(i, j):
                dc = 2 * i + j
                act.wait_ge(weff_ready, dc + 1)
                act.dma_start(weff_d[bass.ds(dc * P, P), :], we_s[j][:]).then_inc(weff_out[j], 16)

            split_a(0, 0)
            split_a(0, 1)
            act.wait_ge(att_ready, 1)
            act.dma_start(att_d, att[:]).then_inc(att_out, 16)
            with act.Fori(1, DC // 2) as i:
                store(i - 1, 0)
                split_a(i, 0)
                store(i - 1, 1)
                split_a(i, 1)
            store(DC // 2 - 1, 0)
            store(DC // 2 - 1, 1)
            act.wait_ge(att_out, 16)
            act.wait_ge(weff_out[0], 16 * (DC // 2))
            act.wait_ge(weff_out[1], 16 * (DC // 2))

        @block.vector
        def _(dve):
            dve.wait_ge(lora_in, 48)
            nc.vector.tensor_tensor(cs[:], co_s[:], sc_s[:], ALU.mult).then_inc(cs_ready, 1)
            dve.wait_ge(cs_ready, 1)
            for c in range(KC):
                nc.vector.tensor_scalar(b_sc[:, c, :], b_in_s[:, c, :], cs[:, c:c + 1], None,
                                        ALU.mult).then_inc(bsc_ready, 1)
            dve.wait_ge(lg_mm, 1)
            nc.vector.tensor_tensor(logits[:], ps_lg, b2_s[:], ALU.add).then_inc(lg_ready, 1)
            dve.wait_ge(lg_ready, 1)
            nc.vector.reduce_max(peak[:], logits[:], AX.X).then_inc(sm_step, 1)
            dve.wait_ge(sm_step, 1)
            nc.vector.tensor_scalar(logits[:], logits[:], peak[:], None, ALU.subtract).then_inc(peak_ready, 1)
            dve.wait_ge(exp_ready, 1)
            nc.vector.reduce_sum(total[:], expo[:], AX.X).then_inc(sm_step, 1)
            dve.wait_ge(sm_step, 2)
            nc.vector.reciprocal(inverse[:], total[:]).then_inc(sm_step, 1)
            dve.wait_ge(sm_step, 3)
            nc.vector.tensor_scalar(att[:], expo[:], inverse[:], None, ALU.mult).then_inc(att_ready, 1)
            for c in range(KC):
                dve.wait_ge(bhi_ready, c + 1)
                nc.vector.tensor_tensor(b_lo[:, c, :], b_sc[:, c, :], fp32(b_hi[:, c, :]),
                                        ALU.subtract).then_inc(blo_ready, 1)

            def split_a(i, j):
                dc = 2 * i + j
                dve.wait_ge(ahi_ready, dc + 1)
                nc.vector.tensor_tensor(a_lo[j][:], a_s[j][:], fp32(a_hi[j][:]), ALU.subtract).then_inc(alo_ready, 1)

            def add(i, j):
                dc = 2 * i + j
                dve.wait_ge(weff_mm, dc + 1)
                wait(dve, weff_out[j], 16 * i)
                nc.vector.tensor_tensor(we_s[j][:], acc[:, j, :, :].rearrange("p a b -> p (a b)"), wt_s[j][:],
                                        ALU.add).then_inc(weff_ready, 1)

            def pair(i):
                split_a(i, 0)
                add(i - 1, 1)
                split_a(i, 1)
                add(i, 0)

            split_a(0, 0)
            split_a(0, 1)
            add(0, 0)
            pair(1)
            with dve.Fori(2, DC // 2) as i:
                pair(i)
            add(DC // 2 - 1, 1)


def layer0_block(nc, half, x, cond_w, bias_k, att_d, weff_d, bias, u_d, x1_d):
    first = half == 0
    with ExitStack() as ctx:
        def sb(name, shape, dt=F32):
            return ctx.enter_context(nc.sbuf_tensor(f"{name}_h{half}", shape, dt))

        def sem(name):
            return ctx.enter_context(nc.semaphore(f"{name}_h{half}"))

        XW = L if first else HALF
        NU = 1 if first else 2
        w_hi, w_lo = sb("w_hi", [P, DC, HALF], F32R), sb("w_lo", [P, DC, HALF], F32R)
        u_hi = [sb(f"u_hi{j}", [P, DC, P], F32R) for j in range(2)]
        u_lo = [sb(f"u_lo{j}", [P, DC, P], F32R) for j in range(2)]
        x_s = [sb(f"x_s{j}", [P, XW]) for j in range(2)]
        u_s = [sb(f"u_s{j}", [P, DC, P]) for j in range(NU)]
        x1_s = [sb(f"x1_s{j}", [P, S, HALF // S]) for j in range(2)]
        bias_s = sb("bias_s", [P, HALF])
        if first:
            kern = sb("kern", [P, K, 2 * P])
            att_s = sb("att_s", [P, NB * K])
            agg = [sb(f"agg{j}", [P, 2 * P]) for j in range(2)]
        ps_u = ctx.enter_context(nc.psum_tensor(f"ps_u{half}", [P, DC, P], F32))
        ps_g = ctx.enter_context(nc.psum_tensor(f"ps_g{half}", [P, 2, HALF], F32))
        spare = x_s[1] if first else u_s[1][:].rearrange("p a b -> p (a b)")
        stages = [x1_s[0][:].rearrange("p s q -> p (s q)"), x1_s[1][:].rearrange("p s q -> p (s q)"),
                  spare[:, 0:HALF], spare[:, HALF:L]]
        WIDE = 8

        def stage(dc):
            return dc % 4 if dc < WIDE else dc % 2

        def before(dc):
            return max([c + 1 for c in range(dc) if stage(c) == stage(dc)], default=0)

        w_in = [sem(f"w_in{j}") for j in range(4)]
        whi_ready, wlo_ready = sem("whi_ready"), sem("wlo_ready")
        const_in = sem("const_in")
        x_in = [sem(f"x_in{j}") for j in range(2)]
        u_in = [sem(f"u_in{j}") for j in range(2)]
        u_out = sem("u_out")
        agg_step, u_mm, u_ready, uhi_ready, ulo_ready = (sem(n) for n in (
            "agg_step", "u_mm", "u_ready", "uhi_ready", "ulo_ready"))
        gemm, xb_ready, x1_ready = sem("gemm"), sem("xb_ready"), sem("x1_ready")
        x1_out = [sem(f"x1_out{j}") for j in range(2)]
        block = ctx.enter_context(nc.Block())
        PAIRS = NB // 2
        at = half * HALF

        @block.sync
        def _(sp):
            def load_w(dc):
                s = stage(dc)
                wait(sp, whi_ready, before(dc))
                wait(sp, wlo_ready, before(dc))
                sp.dma_start(stages[s], weff_d[dc * P:(dc + 1) * P, at:at + HALF]).then_inc(w_in[s], 16)

            def load_x(i, j):
                n = 2 * i + j
                wait(sp, xb_ready, n - 1)
                if first:
                    wait(sp, u_mm, n - 1)
                sp.dma_start(x_s[j][:], x[n, :, at:at + XW]).then_inc(x_in[j], 16)

            def load_u(i, j):
                n = 2 * i + j
                wait(sp, uhi_ready, n - 1)
                wait(sp, ulo_ready, n - 1)
                sp.dma_start(u_s[j][:], u_d[n, :, :]).then_inc(u_in[j], 16)

            if first:
                sp.dma_start(kern[:, :, 0:P], cond_w).then_inc(const_in, 16)
                sp.dma_start(kern[:, :, P:2 * P],
                             bias_k.rearrange("(a k) o -> a k o", a=1).to_broadcast([P, K, P])).then_inc(const_in, 16)
                sp.dma_start(att_s[:], att_d.rearrange("b k -> (b k)").rearrange("(a n) -> a n", a=1)
                             .to_broadcast([P, NB * K])).then_inc(const_in, 16)
            sp.dma_start(bias_s[:], bias.rearrange("(a n) -> a n", a=1)[:, at:at + HALF]
                         .to_broadcast([P, HALF])).then_inc(const_in, 16)
            load_x(0, 0)
            if not first:
                load_u(0, 0)
            for dc in range(WIDE):
                load_w(dc)
            sp.wait_ge(whi_ready, WIDE)
            sp.wait_ge(wlo_ready, WIDE)
            load_x(0, 1)
            if not first:
                load_u(0, 1)
            for dc in range(WIDE, DC):
                load_w(dc)
            with sp.Fori(1, PAIRS) as i:
                for j in range(2):
                    if not first:
                        load_u(i, j)
                    load_x(i, j)

        @block.gpsimd
        def _(pool):
            def residual(i, j):
                n = 2 * i + j
                pool.wait_ge(x_in[j], 16 * i + 16)
                wait(pool, x1_out[j], 16 * i)
                nc.gpsimd.tensor_tensor(x1_s[j][:].rearrange("p s q -> p q s"),
                                        x_s[j][:, 0:HALF].rearrange("p (q s) -> p q s", s=S),
                                        bias_s[:].rearrange("p (q s) -> p q s", s=S), ALU.add).then_inc(xb_ready, 1)

            pool.wait_ge(const_in, 64 if first else 16)
            pool.wait_ge(whi_ready, DC)
            pool.wait_ge(wlo_ready, DC)
            residual(0, 0)
            residual(0, 1)
            with pool.Fori(1, PAIRS) as i:
                residual(i, 0)
                residual(i, 1)

        @block.tensor
        def _(pe):
            def make_u(i, j):
                n = 2 * i + j
                pe.wait_ge(x_in[j], 16 * i + 16)
                pe.wait_ge(agg_step, K * (n + 1))
                wait(pe, u_ready, n)
                for dc in range(DC):
                    mm = nc.tensor.matmul(ps_u[:, dc, :], x_s[j][:, dc * P:(dc + 1) * P], agg[j][:, 0:P],
                                          start=True, stop=True)
                mm.then_inc(u_mm, 1)

            def products(i, j, opening=False, following=None):
                n = 2 * i + j
                pe.wait_ge(uhi_ready, n + 1)
                pe.wait_ge(ulo_ready, n + 1)
                wait(pe, x1_ready, n - 1)
                for dc in range(DC):
                    if opening:
                        pe.wait_ge(whi_ready, dc + 1)
                        pe.wait_ge(wlo_ready, dc + 1)
                    for u, w in ((u_hi, w_hi), (u_hi, w_lo), (u_lo, w_hi)):
                        for c in range(2):
                            mm = nc.tensor.matmul(ps_g[:, j, c * 512:(c + 1) * 512], u[j][:, dc, :],
                                                  w[:, dc, c * 512:(c + 1) * 512],
                                                  start=(dc == 0 and u is u_hi and w is w_hi),
                                                  stop=(dc == DC - 1 and u is u_lo))
                    if dc == DC // 2 - 1 and following is not None and first:
                        make_u(*following)
                mm.then_inc(gemm, 1)

            if first:
                make_u(0, 0)
            products(0, 0, True, (0, 1))
            products(0, 1, False, (1, 0))
            with pe.Fori(1, PAIRS - 1) as i:
                products(i, 0, False, (i, 1))
                products(i, 1, False, (i + 1, 0))
            products(PAIRS - 1, 0, False, (PAIRS - 1, 1))
            products(PAIRS - 1, 1)

        @block.scalar
        def _(act):
            def split_w(dc):
                s = stage(dc)
                uses = sum(1 for c in range(dc + 1) if stage(c) == s)
                act.wait_ge(w_in[s], 16 * uses)
                nc.scalar.activation(w_hi[:, dc, :], stages[s], ACT.Copy).then_inc(whi_ready, 1)

            def split_u(i, j):
                n = 2 * i + j
                if first:
                    act.wait_ge(u_ready, n + 1)
                    act.dma_start(u_d[n, :, :], u_s[0][:]).then_inc(u_out, 16)
                else:
                    act.wait_ge(u_in[j], 16 * i + 16)
                wait(act, gemm, n - 1)
                nc.scalar.activation(u_hi[j][:], u_s[0 if first else j][:], ACT.Copy).then_inc(uhi_ready, 1)

            def store(i, j):
                n = 2 * i + j
                act.wait_ge(x1_ready, n + 1)
                act.dma_start(x1_d[n, :, :, at // S:(at + HALF) // S], x1_s[j][:]).then_inc(x1_out[j], 16)

            split_u(0, 0)
            for dc in range(DC):
                split_w(dc)
            split_u(0, 1)
            store(0, 0)
            with act.Fori(1, PAIRS) as i:
                split_u(i, 0)
                store(i - 1, 1)
                split_u(i, 1)
                store(i, 0)
            store(PAIRS - 1, 1)
            if first:
                act.wait_ge(u_out, 16 * NB)
            act.wait_ge(x1_out[0], 16 * PAIRS)
            act.wait_ge(x1_out[1], 16 * PAIRS)

        @block.vector
        def _(dve):
            def aggregate(i, j):
                n = 2 * i + j
                wait(dve, u_mm, n - 1)
                for k in range(K):
                    w = att_s[:, bass.ds(K * n + k, 1)]
                    if k == 0:
                        op = nc.vector.tensor_scalar(agg[j][:], kern[:, 0, :], w, None, ALU.mult)
                    else:
                        dve.wait_ge(agg_step, K * n + k)
                        op = nc.vector.scalar_tensor_tensor(out=agg[j][:], in0=kern[:, k, :], scalar=w,
                                                            in1=agg[j][:], op0=ALU.mult, op1=ALU.add)
                    op.then_inc(agg_step, 1)

            def take_u(i, j):
                n = 2 * i + j
                if first:
                    dve.wait_ge(u_mm, n + 1)
                    dve.wait_ge(agg_step, K * (n + 1))
                    wait(dve, uhi_ready, n)
                    wait(dve, ulo_ready, n)
                    wait(dve, u_out, 16 * n)
                    nc.vector.tensor_tensor(u_s[0][:], ps_u[:],
                                            agg[j][:, P:2 * P].unsqueeze(1).to_broadcast([P, DC, P]),
                                            ALU.add).then_inc(u_ready, 1)
                dve.wait_ge(uhi_ready, n + 1)
                wait(dve, gemm, n - 1)
                nc.vector.tensor_tensor(u_lo[j][:], u_s[0 if first else j][:], fp32(u_hi[j][:]),
                                        ALU.subtract).then_inc(ulo_ready, 1)

            def take_x1(i, j):
                n = 2 * i + j
                dve.wait_ge(gemm, n + 1)
                dve.wait_ge(xb_ready, n + 1)
                x1 = x1_s[j][:].rearrange("p s q -> p q s")
                nc.vector.tensor_tensor(x1, ps_g[:, j, :].rearrange("p (q s) -> p q s", s=S), x1,
                                        ALU.add).then_inc(x1_ready, 1)

            if first:
                dve.wait_ge(const_in, 64)
                aggregate(0, 0)
                take_u(0, 0)
                aggregate(0, 1)
            else:
                take_u(0, 0)
            for dc in range(DC):
                dve.wait_ge(whi_ready, dc + 1)
                nc.vector.tensor_tensor(w_lo[:, dc, :], stages[stage(dc)], fp32(w_hi[:, dc, :]),
                                        ALU.subtract).then_inc(wlo_ready, 1)
            take_u(0, 1)
            if first:
                aggregate(1, 0)
            take_x1(0, 0)
            with dve.Fori(1, PAIRS - 1) as i:
                take_u(i, 0)
                if first:
                    aggregate(i, 1)
                take_x1(i - 1, 1)
                take_u(i, 1)
                if first:
                    aggregate(i + 1, 0)
                take_x1(i, 0)
            take_u(PAIRS - 1, 0)
            if first:
                aggregate(PAIRS - 1, 1)
            take_x1(PAIRS - 2, 1)
            take_u(PAIRS - 1, 1)
            take_x1(PAIRS - 1, 0)
            take_x1(PAIRS - 1, 1)


def layer1_block(nc, x1_d, cond_t, conv_w, ctx_w, fside, up, down, perm, ident, z_d, y_d, out):
    with ExitStack() as ctx:
        def sb(name, shape, dt=F32):
            return ctx.enter_context(nc.sbuf_tensor(name, shape, dt))

        def sem(name):
            return ctx.enter_context(nc.semaphore(name))

        def bank(name, n=1):
            return ctx.enter_context(nc.psum_tensor(name, [P, n, 512], F32))

        up_hi, up_lo = sb("up_hi", [P, H, M], F32R), sb("up_lo", [P, H, M], F32R)
        dn_hi, dn_lo = sb("dn_hi", [P, H, MC * P], F32R), sb("dn_lo", [P, H, MC * P], F32R)
        cw_hi, cw_lo = sb("cw_hi", [P, G * 3, P], F32R), sb("cw_lo", [P, G * 3, P], F32R)
        xp = [sb(f"xp{j}", [P, Q + 2]) for j in range(2)]
        xp_hi, xp_lo = sb("xp_hi", [P, Q + 2], F32R), sb("xp_lo", [P, Q + 2], F32R)
        z_s = sb("z_s", [P, Q])
        zt_s = sb("zt_s", [P, 4, S, C])
        t_s = [sb(f"t_s{j}", [P, RB]) for j in range(2)]
        t_hi, t_lo = sb("t_hi", [P, RB], F32R), sb("t_lo", [P, RB], F32R)
        g_s = sb("g_s", [P, 2, 2 * RB])
        g_hi = [sb(f"g_hi{c}", [P, 2, RB], F32R) for c in range(2)]
        g_lo = [sb(f"g_lo{c}", [P, 2, RB], F32R) for c in range(2)]
        y_s = [sb(f"y_s{j}", [P, RB]) for j in range(2)]
        yt_s = [sb(f"yt_s{j}", [P, 4, C]) for j in range(2)]
        x1_s = [sb(f"x1f_s{j}", [P, S, P]) for j in range(2)]
        o_s = [sb(f"o_s{j}", [P, 512]) for j in range(2)]
        idx = sb("idx", [P, H], I32)
        id_s = sb("id_s", [P, P])
        cbias = sb("cbias", [P, G, NB])
        fs_s = sb("fs_s", [P, G])

        ps_up = [bank(f"ps_up{c}", 2) for c in range(2)]
        ps_c, ps_zt, ps_y, ps_f = bank("ps_c"), bank("ps_zt"), bank("ps_y"), bank("ps_f")

        small_in, cw_in, cw_zero, w_in = sem("small_in"), sem("cw_in"), sem("cw_zero"), [sem(f"l1w_in{j}") for j in range(2)]
        pad_ready, ctx_mm, cbias_ready = sem("pad_ready"), sem("ctx_mm"), sem("cbias_ready")
        wsplit_hi, wsplit_lo = sem("wsplit_hi"), sem("wsplit_lo")
        xp_in = [sem(f"xp_in{j}") for j in range(2)]
        xhi_ready, xlo_ready, conv_done, z_ready, zt_done, zt_ready, z_out = (sem(n) for n in (
            "xhi_ready", "xlo_ready", "conv_done", "z_ready", "zt_done", "zt_ready", "z_out"))
        t_in = [sem(f"t_in{j}") for j in range(2)]
        thi_ready, tlo_ready, up_done, gelu_done, ghi_ready, glo_ready, down_done, y_ready = (sem(n) for n in (
            "thi_ready", "tlo_ready", "up_done", "gelu_done", "ghi_ready", "glo_ready", "down_done", "y_ready"))
        gather_clear, scatter_clear = sem("gather_clear"), sem("scatter_clear")
        block_scattered, block_gathered = sem("block_scattered"), sem("block_gathered")
        y_out = [sem(f"y_out{j}") for j in range(2)]
        yt_in = [sem(f"yt_in{j}") for j in range(2)]
        x1_in = [sem(f"x1f_in{j}") for j in range(2)]
        fin_done, o_ready = sem("fin_done"), sem("o_ready")
        o_out = [sem(f"o_out{j}") for j in range(2)]
        block = ctx.enter_context(nc.Block())

        STEPS = BLOCKS * H
        CW = G * 3 * P
        stage = [g_s[:, 0, :], g_s[:, 1, :]]
        cw_stage = g_s[:].rearrange("p c n -> p (c n)")[:, 0:CW]
        chunks = []
        for h in range(0, H, 2):
            chunks.append((up_hi[:, h:h + 2, :], up_lo[:, h:h + 2, :], up[:, h:h + 2, :]))
        for h in range(0, H, 2):
            chunks.append((dn_hi[:, h:h + 2, :], dn_lo[:, h:h + 2, :], down[:, h:h + 2, :]))

        def has_conv(k, h):
            return not isinstance(k, int) or H * k + h + LEAD < STEPS

        def has_final(k):
            return not isinstance(k, int) or 1 <= k <= BLOCKS

        def has_mlp(k):
            return not isinstance(k, int) or 0 <= k < BLOCKS

        def drive(eng, step):
            for h in range(2 * H - LEAD, H):
                step(-2, h, 0)
            for k in (-1, 0, 1):
                for h in range(H):
                    step(k, h, k % 2)
            with eng.Fori(1, BLOCKS // 2 - 1) as i:
                for parity in range(2):
                    for h in range(H):
                        step(2 * i + parity, h, parity)
            for k in (BLOCKS - 2, BLOCKS - 1, BLOCKS):
                for h in range(H):
                    step(k, h, k % 2)

        def conv_unit(k, h):
            return H * k + h + LEAD, h % 2, SB * k + (h + LEAD) // G, h % G

        def final_unit(k, h):
            return H * (k - 1) + h, h % 2, SB * (k - 1) + h // 4, h % 4

        @block.sync
        def _(sp):
            sp.dma_start(t_s[0][:, 0:C], ctx_w).then_inc(small_in, 16)
            sp.dma_start(t_s[1][:, 0:NB], cond_t).then_inc(small_in, 16)
            sp.dma_start(idx[:], perm).then_inc(small_in, 16)
            sp.dma_start(id_s[:], ident).then_inc(small_in, 16)
            for r in range(S):
                sp.dma_start(fs_s[r * GC:(r + 1) * GC, :], fside, allow_slow_non_contiguous=True).then_inc(small_in, 16)
            sp.wait_ge(cw_zero, 1)
            for s in range(S):
                for tau in (-1, 0, 1):
                    lo, hi = max(0, 4 * tau + s - 4), min(S - 1, 4 * tau + s + 4)
                    kr = 4 - 4 * tau - s + lo
                    n = hi - lo + 1
                    dst = cw_stage[s * GC:(s + 1) * GC, :].rearrange("p (g m) -> p g m", g=G)
                    off = (tau + 1) * P + lo * GC
                    sp.dma_start(dst[:, :, off:off + n * GC], conv_w[:, :, kr * GC:(kr + n) * GC]).then_inc(cw_in, 16)
            for n, (_, _, src) in enumerate(chunks):
                sp.wait_ge(wsplit_lo, n if n >= 1 else 1)
                sp.dma_start(stage[n % 2].rearrange("p (a b) -> p a b", a=2), src).then_inc(w_in[n % 2], 16)

            def load_x1(u, j, b, g, after):
                wait(sp, xlo_ready, after)
                for s in range(S):
                    sp.dma_start(xp[j][s * GC:(s + 1) * GC, 1:Q + 1],
                                 x1_d[b, g * GC:(g + 1) * GC, s, :]).then_inc(xp_in[j], 16)

            def load_final(k, h, parity):
                v, j, b, c = final_unit(k, h)
                if h == 0:
                    scattered = 16 * (H // 2) * k
                    if not isinstance(k, int):
                        scattered = sp.snap(scattered)
                    wait(sp, y_out[0], scattered)
                    wait(sp, y_out[1], scattered)
                    sp.sem_inc(block_scattered, 1)
                wait(sp, fin_done, v - 1)
                sp.dma_start(yt_s[j][:], y_d[1 - parity][c * 512:(c + 1) * 512, h // 4 * C:(h // 4 + 1) * C]
                             .rearrange("(l p) r -> p l r", p=P)).then_inc(yt_in[j], 16)
                wait(sp, o_ready, v - 1)
                sp.dma_start(x1_s[j][:], x1_d[b, :, :, c * P:(c + 1) * P]).then_inc(x1_in[j], 16)

            def store_out(k, h):
                v, j, b, c = final_unit(k, h)
                sp.wait_ge(o_ready, v + 1)
                sp.dma_start(out[b, :, c * 512:(c + 1) * 512], o_s[j][:]).then_inc(o_out[j], 16)

            def store_z(k, h, parity):
                u = conv_unit(k, h)[0]
                jb = ((h + LEAD) // G - 1) % SB
                ahead = ((h + LEAD) // G - 1) // SB
                if jb == 0:
                    wait(sp, tlo_ready, H * (k + ahead - 1))
                    sp.sem_inc(block_gathered, 1)
                sp.wait_ge(zt_ready, u)
                for w in range(4):
                    sp.dma_start(z_d[(parity + ahead) % 2][w * 512:(w + 1) * 512, jb * C:(jb + 1) * C]
                                 .rearrange("(q r) n -> q r n", r=S), zt_s[:, w, :, :]).then_inc(z_out, 16)

            def step(k, h, parity):
                if has_conv(k, h):
                    u, j, b, g = conv_unit(k, h)
                    load_x1(u, j, b, g, u - 1)
                if has_final(k):
                    load_final(k, h, parity)
                    if h or not (isinstance(k, int) and k == 1):
                        store_out(*((k, h - 1) if h else (k - 1, H - 1)))
                if h % G == 0 and (has_conv(k, h) or (isinstance(k, int) and H * k + h + LEAD == STEPS)) \
                        and not (isinstance(k, int) and H * k + h + LEAD == 0):
                    store_z(k, h, parity)

            sp.wait_ge(pad_ready, 2)
            drive(sp, step)
            store_out(BLOCKS, H - 1)
            sp.wait_ge(o_out[0], 16 * (STEPS // 2))
            sp.wait_ge(o_out[1], 16 * (STEPS // 2))

        @block.gpsimd
        def _(pool):
            nc.gpsimd.memset(cw_stage, 0.0).then_inc(cw_zero, 1)
            nc.gpsimd.memset(xp[0][:], 0.0).then_inc(pad_ready, 1)
            nc.gpsimd.memset(xp[1][:], 0.0).then_inc(pad_ready, 1)

            def gather(k, h, parity):
                s, j = H * k + h, h % 2
                if h == 0:
                    pool.wait_ge(z_out, 64 * SB * (k + 1))
                wait(pool, tlo_ready, s - 1)
                pool.sem_inc(gather_clear, 1)
                nc.gpsimd.indirect_dma_start(
                    out=t_s[j][:], out_offset=None, in_=z_d[parity],
                    in_offset=bass.IndirectOffsetOnAxis(ap=idx[:, h:h + 1], axis=0)).then_inc(t_in[j], 16)

            def step(k, h, parity):
                if has_mlp(k):
                    if isinstance(k, int) and k == 0 and h == 0:
                        pool.wait_ge(small_in, 128)
                        pool.wait_ge(cbias_ready, 1)
                        gather(0, 0, 0)
                    if h < H - 1:
                        gather(k, h + 1, parity)
                    elif has_mlp(k + 1):
                        gather(k + 1, 0, 1 - parity)
                    s, j = H * k + h, h % 2
                    pool.wait_ge(y_ready, s + 1)
                    if h == 0:
                        wait(pool, yt_in[0], 16 * (H // 2) * (k - 1))
                        wait(pool, yt_in[1], 16 * (H // 2) * (k - 1))
                    pool.sem_inc(scatter_clear, 1)
                    nc.gpsimd.indirect_dma_start(
                        out=y_d[parity], out_offset=bass.IndirectOffsetOnAxis(ap=idx[:, h:h + 1], axis=0),
                        in_=y_s[j][:], in_offset=None).then_inc(y_out[j], 16)

            drive(pool, step)
            pool.wait_ge(y_out[0], 16 * (STEPS // 2))
            pool.wait_ge(y_out[1], 16 * (STEPS // 2))

        @block.tensor
        def _(pe):
            pe.wait_ge(small_in, 128)
            for g in range(G):
                for r in range(S):
                    mm = nc.tensor.matmul(ps_c[r * GC:(r + 1) * GC, 0, g * NB:(g + 1) * NB],
                                          t_s[0][:, g * GC:(g + 1) * GC], t_s[1][:, 0:NB], start=True, stop=True)
            mm.then_inc(ctx_mm, 1)

            def up_part(k, h, c):
                s = H * k + h
                if c == 0:
                    pe.wait_ge(tlo_ready, s + 1)
                wait(pe, gelu_done, 2 * s - 1 + c)
                for m in range(2):
                    mc = 2 * c + m
                    for w, t in ((up_hi, t_hi), (up_hi, t_lo), (up_lo, t_hi)):
                        mm = nc.tensor.matmul(ps_up[c][:, m, :], w[:, h, mc * P:(mc + 1) * P], t[:],
                                              start=(w is up_hi and t is t_hi), stop=(w is up_lo))
                mm.then_inc(up_done, 1)

            def down_part(k, h, c):
                s = H * k + h
                pe.wait_ge(glo_ready, 2 * s + c + 1)
                if c == 0:
                    wait(pe, y_ready, s)
                for m in range(2):
                    mc = 2 * c + m
                    for w, g in ((dn_hi, g_hi), (dn_hi, g_lo), (dn_lo, g_hi)):
                        mm = nc.tensor.matmul(ps_y[:, 0, :], w[:, h, mc * P:(mc + 1) * P], g[c][:, m, :],
                                              start=(mc == 0 and w is dn_hi and g is g_hi),
                                              stop=(mc == MC - 1 and w is dn_lo))
                mm.then_inc(down_done, 1)

            def conv(k, h):
                u, j, b, g = conv_unit(k, h)
                pe.wait_ge(xlo_ready, u + 1)
                wait(pe, z_ready, u)
                for tau in range(3):
                    for w, x in ((cw_hi, xp_hi), (cw_hi, xp_lo), (cw_lo, xp_hi)):
                        mm = nc.tensor.matmul(ps_c[:, 0, :], w[:, 3 * g + tau, :], x[:, tau:tau + Q],
                                              start=(tau == 0 and w is cw_hi and x is xp_hi),
                                              stop=(tau == 2 and w is cw_lo))
                mm.then_inc(conv_done, 1)

            def turn_z(k, h):
                u, _, _, _ = conv_unit(k, h)
                pe.wait_ge(z_ready, u + 1)
                wait(pe, zt_ready, u)
                for w in range(4):
                    mm = nc.tensor.transpose(ps_zt[:, 0, w * P:(w + 1) * P], z_s[:, w * P:(w + 1) * P], id_s[:])
                mm.then_inc(zt_done, 1)

            def turn_y(k, h):
                v, j, _, _ = final_unit(k, h)
                pe.wait_ge(yt_in[j], 16 * (H // 2 * (k - 1) + h // 2 + 1))
                wait(pe, o_ready, v)
                for l in range(4):
                    mm = nc.tensor.transpose(ps_f[:, 0, l * P:(l + 1) * P], yt_s[j][:, l, :], id_s[:])
                mm.then_inc(fin_done, 1)

            pe.wait_ge(cbias_ready, 1)
            pe.wait_ge(wsplit_lo, 1)

            def step(k, h, parity):
                if has_mlp(k):
                    if isinstance(k, int) and k == 0 and h == 0:
                        pe.wait_ge(wsplit_lo, 1 + len(chunks))
                    up_part(k, h, 0)
                    up_part(k, h, 1)
                if has_conv(k, h):
                    conv(k, h)
                if has_mlp(k):
                    down_part(k, h, 0)
                    down_part(k, h, 1)
                if has_conv(k, h):
                    turn_z(k, h)
                if has_final(k):
                    turn_y(k, h)

            drive(pe, step)

        @block.scalar
        def _(act):
            act.wait_ge(cw_in, 16 * 12)
            nc.scalar.activation(cw_hi[:].rearrange("p a b -> p (a b)"), cw_stage, ACT.Copy).then_inc(wsplit_hi, 1)
            for n, (hi, _, _) in enumerate(chunks):
                act.wait_ge(w_in[n % 2], 16 * (n // 2 + 1))
                nc.scalar.activation(hi, stage[n % 2].rearrange("p (a b) -> p a b", a=2), ACT.Copy).then_inc(wsplit_hi, 1)

            def split_x(k, h):
                u, j, _, _ = conv_unit(k, h)
                act.wait_ge(xp_in[j], 64 * (H // 2 * k + (h + LEAD) // 2 + 1))
                wait(act, conv_done, u)
                nc.scalar.activation(xp_hi[:], xp[j][:], ACT.Copy).then_inc(xhi_ready, 1)

            def split_t(k, h):
                s, j = H * k + h, h % 2
                act.wait_ge(t_in[j], 16 * (H // 2 * k + h // 2 + 1))
                wait(act, up_done, 2 * s)
                nc.scalar.activation(t_hi[:], t_s[j][:], ACT.Copy).then_inc(thi_ready, 1)

            def after(k, h):
                return (k, h + 1) if h < H - 1 else (k + 1, 0)

            act.wait_ge(pad_ready, 2)
            act.wait_ge(cbias_ready, 1)
            split_x(-2, 2 * H - LEAD)

            def step(k, h, parity):
                if has_mlp(k):
                    s, j = H * k + h, h % 2
                    if isinstance(k, int) and k == 0 and h == 0:
                        split_t(0, 0)
                        act.wait_ge(wsplit_lo, 1 + len(chunks))
                    for c in range(2):
                        act.wait_ge(up_done, 2 * s + c + 1)
                        wait(act, glo_ready, 2 * s - 1 + c)
                        nc.scalar.activation(g_s[:, c, :].rearrange("p (m n) -> p m n", m=2), ps_up[c][:],
                                             ACT.Gelu).then_inc(gelu_done, 1)
                    if has_mlp(after(k, h)[0]):
                        split_t(*after(k, h))
                if has_conv(k, h):
                    u, j, b, g = conv_unit(k, h)
                    act.wait_ge(conv_done, u + 1)
                    wait(act, zt_done, u)
                    nc.scalar.activation(z_s[:], ps_c[:, 0, :], ACT.Identity,
                                         bias=cbias[:, g, bass.ds(b, 1)]).then_inc(z_ready, 1)
                    if has_conv(*after(k, h)):
                        split_x(*after(k, h))
                if has_mlp(k):
                    s, j = H * k + h, h % 2
                    act.wait_ge(down_done, 2 * s + 2)
                    wait(act, y_out[j], 16 * (H // 2 * k + h // 2))
                    nc.scalar.activation(y_s[j][:], ps_y[:, 0, :], ACT.Copy).then_inc(y_ready, 1)

            drive(act, step)

        @block.vector
        def _(dve):
            dve.wait_ge(small_in, 128)
            dve.wait_ge(ctx_mm, 1)
            nc.vector.tensor_tensor(cbias[:], ps_c[:, 0, 0:G * NB].rearrange("p (g b) -> p g b", g=G),
                                    fs_s[:].unsqueeze(2).to_broadcast([P, G, NB]), ALU.add).then_inc(cbias_ready, 1)
            dve.wait_ge(wsplit_hi, 1)
            nc.vector.tensor_tensor(cw_lo[:].rearrange("p a b -> p (a b)"), cw_stage,
                                    fp32(cw_hi[:].rearrange("p a b -> p (a b)")), ALU.subtract).then_inc(wsplit_lo, 1)
            for n, (hi, lo, _) in enumerate(chunks):
                dve.wait_ge(wsplit_hi, n + 2)
                nc.vector.tensor_tensor(lo, stage[n % 2].rearrange("p (a b) -> p a b", a=2), fp32(hi),
                                        ALU.subtract).then_inc(wsplit_lo, 1)

            def split_x(k, h):
                u, j, _, _ = conv_unit(k, h)
                dve.wait_ge(xhi_ready, u + 1)
                wait(dve, conv_done, u)
                nc.vector.tensor_tensor(xp_lo[:], xp[j][:], fp32(xp_hi[:]), ALU.subtract).then_inc(xlo_ready, 1)

            def split_t(k, h):
                s, j = H * k + h, h % 2
                dve.wait_ge(thi_ready, s + 1)
                wait(dve, up_done, 2 * s)
                nc.vector.tensor_tensor(t_lo[:], t_s[j][:], fp32(t_hi[:]), ALU.subtract).then_inc(tlo_ready, 1)

            def after(k, h):
                return (k, h + 1) if h < H - 1 else (k + 1, 0)

            split_x(-2, 2 * H - LEAD)

            def step(k, h, parity):
                if has_mlp(k):
                    s = H * k + h
                    if isinstance(k, int) and k == 0 and h == 0:
                        split_t(0, 0)
                    for c in range(2):
                        dve.wait_ge(gelu_done, 2 * s + c + 1)
                        wait(dve, down_done, 2 * s - 1 + c)
                        g = g_s[:, c, :].rearrange("p (m n) -> p m n", m=2)
                        nc.vector.tensor_copy(g_hi[c][:], g).then_inc(ghi_ready, 1)
                        dve.wait_ge(ghi_ready, 2 * s + c + 1)
                        nc.vector.tensor_tensor(g_lo[c][:], g, fp32(g_hi[c][:]), ALU.subtract).then_inc(glo_ready, 1)
                    if has_mlp(after(k, h)[0]):
                        split_t(*after(k, h))
                if has_conv(k, h) and has_conv(*after(k, h)):
                    split_x(*after(k, h))
                if has_conv(k, h):
                    u, j, b, g = conv_unit(k, h)
                    dve.wait_ge(zt_done, u + 1)
                    if g == 0:
                        wait(dve, z_out, 64 * b)
                    nc.vector.tensor_copy(zt_s[:, :, :, g * GC:(g + 1) * GC],
                                          ps_zt[:, 0, :].rearrange("p (w r o) -> p w r o", w=4, r=S)).then_inc(zt_ready, 1)
                if has_final(k):
                    v, j, b, c = final_unit(k, h)
                    n = H // 2 * (k - 1) + h // 2
                    dve.wait_ge(fin_done, v + 1)
                    dve.wait_ge(x1_in[j], 16 * (n + 1))
                    wait(dve, o_out[j], 16 * n)
                    nc.vector.tensor_tensor(o_s[j][:].rearrange("p (q s) -> p q s", s=S),
                                            ps_f[:, 0, :].rearrange("p (q s) -> p q s", s=S),
                                            x1_s[j][:].rearrange("p s q -> p q s"), ALU.add).then_inc(o_ready, 1)

            drive(dve, step)


def build(nc, x, cond_t, fside, w0, b0, w1, b1, w2, b2, cond_w, bias_k, w_t, bias, lora_a, lora_b, coeffs, scales,
          conv_w, ctx_w, up, down, perm, ident, out):
    def scratch(name, shape):
        return nc.dram_tensor(name, shape, F32, kind="Internal").ap()

    att_d = scratch("att_d", [NB, K])
    weff_d = scratch("weff_d", [L, L])
    u_d = scratch("u_d", [NB, P, DC * P])
    x1_d = scratch("x1_d", [NB, C, S, Q])
    z_d = [scratch(f"z_d{j}", [L, RB]) for j in range(2)]
    y_d = [scratch(f"y_d{j}", [L, RB]) for j in range(2)]
    setup_block(nc, cond_t, w0, b0, w1, b1, w2, b2, w_t, lora_a, lora_b, coeffs, scales, att_d, weff_d)
    for half in range(2):
        layer0_block(nc, half, x, cond_w, bias_k, att_d, weff_d, bias, u_d, x1_d)
    layer1_block(nc, x1_d, cond_t, conv_w, ctx_w, fside, up, down, perm, ident, z_d, y_d, out)


def kernel(**inputs):
    import numpy as np
    import concourse.bacc as bacc
    from concourse.bass_utils import run_bass_kernel_spmd

    def v(name):
        return np.asarray(inputs[name])

    def by_partition(a):
        return a.reshape(KC, P).T

    def repeat_rank(a):
        return np.broadcast_to(a[:, None], (16, 16)).reshape(ER)

    arrays = {
        "x": v("x"),
        "cond_t": v("cond_128").T,
        "fside": v("fside_S_0").reshape(G, GC).T,
        "w0": v("L0_cond_W0"), "b0": v("L0_cond_b0"),
        "w1": v("L0_cond_W1"), "b1": v("L0_cond_b1"),
        "w2": v("L0_cond_W2"), "b2": v("L0_cond_b2"),
        "cond_w": v("L0_cond_weight")[..., 0].transpose(2, 0, 1),
        "bias_k": v("L0_cond_bias_k"),
        "w_t": v("L0_ffn_W").T,
        "bias": v("L0_ffn_bias"),
        "lora_a": v("L0_ffn_A").reshape(ER, L),
        "lora_b": v("L0_ffn_Bf").transpose(0, 2, 1).reshape(ER, L),
        "coeffs": by_partition(repeat_rank(v("L0_ffn_coeffs"))),
        "scales": by_partition(repeat_rank(v("L0_ffn_scales"))),
        "conv_w": v("L1_cond_weight").reshape(G, GC, GC, TAPS)[..., ::-1].transpose(2, 0, 3, 1).reshape(GC, G, TAPS * GC),
        "ctx_w": v("L1_cond_c_weight").T,
        "up": v("L1_ffn_up").transpose(1, 0, 2),
        "down": v("L1_ffn_down").reshape(H, MC, P, P).transpose(2, 0, 1, 3).reshape(P, H, MC * P),
        "perm": v("L1_ffn_perm").reshape(H, P).T,
        "ident": np.eye(P, dtype=np.float32),
    }
    nc = bacc.Bacc("TRN2", target_bir_lowering=False, num_devices=1)
    args, feed = [], {}
    for name, a in arrays.items():
        a = np.ascontiguousarray(a)
        feed[f"in_{name}"] = a
        args.append(nc.dram_tensor(f"in_{name}", a.shape, mybir.dt.from_np(a.dtype), kind="ExternalInput").ap())
    out = nc.dram_tensor("out_0_dram", (NB, C, L), F32, kind="ExternalOutput").ap()
    build(nc, *args, out)
    r = run_bass_kernel_spmd(nc, [feed], core_ids=[0])
    return r.results[0]["out_0_dram"]
```

```python
import concourse.bass as bass
from concourse import mybir
from contextlib import ExitStack

F32 = mybir.dt.float32
F32R = mybir.dt.float32r
I32 = mybir.dt.int32
ALU = mybir.AluOpType
ACT = mybir.ActivationFunctionType
AX = mybir.AxisListType

P = 128
NB, C, L = 32, 128, 2048
DC = L // P
HALF = L // 2
K = 8
ER = 256
KC = ER // P
G, GC, TAPS, S = 4, 32, 9, 4
Q = L // S
H, M = 16, 512
MC = M // P
RB = 512
BLOCKS = NB * C // RB
SB = RB // C
LEAD = 20


def wait(eng, sem, value):
    if isinstance(value, int) and value <= 0:
        return
    eng.wait_ge(sem, value)


def fp32(ap):
    return ap.bitcast(F32)


def setup_block(nc, w_hi, w_lo, cond_t, w0, b0, w1, b1, w2, b2, w_t, lora_a, lora_b, coeffs, scales, att_d, weff_d):
    with ExitStack() as ctx:
        def sb(name, shape, dt=F32):
            return ctx.enter_context(nc.sbuf_tensor(name, shape, dt))

        def sem(name):
            return ctx.enter_context(nc.semaphore(name))

        cond_s = sb("cond_s", [P, NB])
        w0_s, w1_s, w2_s = sb("w0_s", [P, P]), sb("w1_s", [P, P]), sb("w2_s", [P, K])
        b0_s, b1_s, b2_s = sb("b0_s", [P, 1]), sb("b1_s", [P, 1]), sb("b2_s", [NB, K])
        h0, h1 = sb("h0", [P, NB]), sb("h1", [P, NB])
        logits, expo, att = sb("logits", [NB, K]), sb("expo", [NB, K]), sb("att", [NB, K])
        peak, total, inverse = sb("peak", [NB, 1]), sb("total", [NB, 1]), sb("inverse", [NB, 1])
        co_s, sc_s, cs = sb("co_s", [P, KC]), sb("sc_s", [P, KC]), sb("cs", [P, KC])
        b_s = sb("b_s", [P, KC, L])
        b_hi, b_lo = sb("b_hi", [P, KC, L], F32R), sb("b_lo", [P, KC, L], F32R)
        a_s = [sb(f"a_s{j}", [P, KC, P]) for j in range(2)]
        a_hi = [sb(f"a_hi{j}", [P, KC, P], F32R) for j in range(2)]
        a_lo = [sb(f"a_lo{j}", [P, KC, P], F32R) for j in range(2)]
        wt_s = [[sb(f"wt_s{j}{half}", [P, HALF]) for half in range(2)] for j in range(2)]
        acc = ctx.enter_context(nc.psum_tensor("acc", [P, 2, 2, HALF], F32))
        ps_h0, ps_h1, ps_lg = acc[:, 1, 1, 0:NB], acc[:, 1, 1, P:P + NB], acc[0:NB, 1, 1, 512:512 + K]

        cond_in, scale_in = sem("cond_in"), sem("scale_in")
        b_in = [sem(f"b_in{c}") for c in range(KC)]
        a_in = [sem(f"a_in{j}") for j in range(2)]
        wt_in = [[sem(f"wt_in{j}{half}") for half in range(2)] for j in range(2)]
        h0_mm, h0_ready, h1_mm, h1_ready = sem("h0_mm"), sem("h0_ready"), sem("h1_mm"), sem("h1_ready")
        lg_mm, lg_ready, peak_ready, exp_ready, att_ready = (sem(n) for n in (
            "lg_mm", "lg_ready", "peak_ready", "exp_ready", "att_ready"))
        sm_step, att_out = sem("sm_step"), sem("att_out")
        cs_ready, bsc_ready, bhi_ready, blo_ready = sem("cs_ready"), sem("bsc_ready"), sem("bhi_ready"), sem("blo_ready")
        ahi_ready, alo_ready, whi_ready, wlo_ready = sem("ahi_ready"), sem("alo_ready"), sem("whi_ready"), sem("wlo_ready")
        item_mm = [sem(f"item_mm{half}") for half in range(2)]
        item_sum = [sem(f"item_sum{half}") for half in range(2)]
        weff_out = [sem(f"weff_out{j}") for j in range(2)]
        block = ctx.enter_context(nc.Block())

        a_v = lora_a.rearrange("(c p) d -> p c d", p=P)

        @block.sync
        def _(sp):
            def load(i, j):
                dc = 2 * i + j
                wait(sp, alo_ready, dc - 1)
                sp.dma_start(a_s[j][:], a_v[:, :, bass.ds(dc * P, P)]).then_inc(a_in[j], 16)
                wait(sp, wlo_ready, dc - 1)
                sp.dma_start(wt_s[j][0][:], w_t[bass.ds(dc * P, P), 0:HALF]).then_inc(wt_in[j][0], 16)
                wait(sp, weff_out[j], 16 * i)
                sp.dma_start(wt_s[j][1][:], w_t[bass.ds(dc * P, P), HALF:L]).then_inc(wt_in[j][1], 16)

            sp.dma_start(co_s[:], coeffs).then_inc(scale_in, 16)
            sp.dma_start(sc_s[:], scales).then_inc(scale_in, 16)
            sp.dma_start(b_s[:, 0, :], lora_b[0:P, :]).then_inc(b_in[0], 16)
            sp.dma_start(b_s[:, 1, :], lora_b[P:2 * P, :]).then_inc(b_in[1], 16)
            load(0, 0)
            load(0, 1)
            with sp.Fori(1, DC // 2) as i:
                load(i, 0)
                load(i, 1)

        @block.tensor
        def _(pe):
            pe.wait_ge(cond_in, 7 * 16)
            nc.tensor.matmul(ps_h0, w0_s[:], cond_s[:], start=True, stop=True).then_inc(h0_mm, 1)
            pe.wait_ge(h0_ready, 1)
            nc.tensor.matmul(ps_h1, w1_s[:], h0[:], start=True, stop=True).then_inc(h1_mm, 1)
            pe.wait_ge(h1_ready, 1)
            nc.tensor.matmul(ps_lg, h1[:], w2_s[:], start=True, stop=True).then_inc(lg_mm, 1)

            def chunk(i, j):
                dc = 2 * i + j
                pe.wait_ge(alo_ready, dc + 1)
                for half in range(2):
                    wait(pe, item_sum[half], dc - 1)
                    if isinstance(dc, int) and dc == 1 and half == 1:
                        pe.wait_ge(lg_ready, 1)
                    for kc in range(KC):
                        if isinstance(dc, int) and dc == 0 and half == 0:
                            pe.wait_ge(blo_ready, kc + 1)
                        for w, b in ((a_hi, b_hi), (a_hi, b_lo), (a_lo, b_hi)):
                            for n in range(2):
                                at = half * HALF + n * 512
                                mm = nc.tensor.matmul(acc[:, j, half, n * 512:(n + 1) * 512], w[j][:, kc, :],
                                                      b[:, kc, at:at + 512],
                                                      start=(kc == 0 and w is a_hi and b is b_hi),
                                                      stop=(kc == KC - 1 and w is a_lo))
                    mm.then_inc(item_mm[half], 1)

            chunk(0, 0)
            chunk(0, 1)
            with pe.Fori(1, DC // 2) as i:
                chunk(i, 0)
                chunk(i, 1)

        @block.scalar
        def _(act):
            for dst, src in ((cond_s, cond_t), (w0_s, w0), (w1_s, w1), (w2_s, w2),
                             (b0_s, b0.rearrange("(p a) -> p a", a=1)), (b1_s, b1.rearrange("(p a) -> p a", a=1)),
                             (b2_s, b2.rearrange("(a k) -> a k", a=1).to_broadcast([NB, K]))):
                act.dma_start(dst[:], src).then_inc(cond_in, 16)
            act.wait_ge(h0_mm, 1)
            nc.scalar.activation(h0[:], ps_h0, ACT.Gelu, bias=b0_s[:]).then_inc(h0_ready, 1)
            act.wait_ge(h1_mm, 1)
            nc.scalar.activation(h1[:], ps_h1, ACT.Gelu, bias=b1_s[:]).then_inc(h1_ready, 1)
            act.wait_ge(bsc_ready, 1)
            nc.scalar.activation(b_hi[:, 0, :], b_s[:, 0, :], ACT.Copy).then_inc(bhi_ready, 1)
            act.wait_ge(bsc_ready, 2)
            nc.scalar.activation(b_hi[:, 1, :], b_s[:, 1, :], ACT.Copy).then_inc(bhi_ready, 1)

            def split_a(i, j):
                dc = 2 * i + j
                act.wait_ge(a_in[j], 16 * i + 16)
                wait(act, item_mm[1], dc - 1)
                nc.scalar.activation(a_hi[j][:], a_s[j][:], ACT.Copy).then_inc(ahi_ready, 1)

            def take(i, j):
                dc = 2 * i + j
                act.wait_ge(item_sum[0], dc + 1)
                nc.scalar.activation(w_hi[:, bass.ds(dc, 1), :].rearrange("p a n -> p (a n)"), wt_s[j][0][:],
                                     ACT.Copy).then_inc(whi_ready, 1)
                act.wait_ge(item_sum[1], dc + 1)
                act.dma_start(weff_d[bass.ds(dc * P, P), :], wt_s[j][1][:]).then_inc(weff_out[j], 16)

            split_a(0, 0)
            split_a(0, 1)
            act.wait_ge(peak_ready, 1)
            nc.scalar.activation(expo[:], logits[:], ACT.Exp).then_inc(exp_ready, 1)
            act.wait_ge(att_ready, 1)
            act.dma_start(att_d, att[:]).then_inc(att_out, 16)
            take(0, 0)

            def pair(i):
                split_a(i, 0)
                take(i - 1, 1)
                split_a(i, 1)
                take(i, 0)

            pair(1)
            with act.Fori(2, DC // 2) as i:
                pair(i)
            take(DC // 2 - 1, 1)
            act.wait_ge(att_out, 16)
            act.wait_ge(weff_out[0], 16 * (DC // 2))
            act.wait_ge(weff_out[1], 16 * (DC // 2))

        @block.vector
        def _(dve):
            dve.wait_ge(scale_in, 32)
            nc.vector.tensor_tensor(cs[:], co_s[:], sc_s[:], ALU.mult).then_inc(cs_ready, 1)
            dve.wait_ge(cs_ready, 1)
            for c in range(KC):
                dve.wait_ge(b_in[c], 16)
                nc.vector.tensor_scalar(b_s[:, c, :], b_s[:, c, :], cs[:, c:c + 1], None,
                                        ALU.mult).then_inc(bsc_ready, 1)
            for c in range(KC):
                dve.wait_ge(bhi_ready, c + 1)
                nc.vector.tensor_tensor(b_lo[:, c, :], b_s[:, c, :], fp32(b_hi[:, c, :]),
                                        ALU.subtract).then_inc(blo_ready, 1)

            def split_a(i, j):
                dc = 2 * i + j
                dve.wait_ge(ahi_ready, dc + 1)
                wait(dve, item_mm[1], dc - 1)
                nc.vector.tensor_tensor(a_lo[j][:], a_s[j][:], fp32(a_hi[j][:]), ALU.subtract).then_inc(alo_ready, 1)

            def add(i, j, half):
                dc = 2 * i + j
                dve.wait_ge(item_mm[half], dc + 1)
                dve.wait_ge(wt_in[j][half], 16 * i + 16)
                nc.vector.tensor_tensor(wt_s[j][half][:], acc[:, j, half, :], wt_s[j][half][:],
                                        ALU.add).then_inc(item_sum[half], 1)

            def split_w(i, j):
                dc = 2 * i + j
                dve.wait_ge(whi_ready, dc + 1)
                here = (slice(None), bass.ds(dc, 1), slice(None))
                nc.vector.tensor_tensor(w_lo[here].rearrange("p a n -> p (a n)"), wt_s[j][0][:],
                                        fp32(w_hi[here].rearrange("p a n -> p (a n)")),
                                        ALU.subtract).then_inc(wlo_ready, 1)

            def chunk(i, j):
                add(i, j, 0)
                add(i, j, 1)
                split_w(i, j)

            split_a(0, 0)
            split_a(0, 1)
            dve.wait_ge(lg_mm, 1)
            nc.vector.tensor_tensor(logits[:], ps_lg, b2_s[:], ALU.add).then_inc(lg_ready, 1)
            dve.wait_ge(lg_ready, 1)
            nc.vector.reduce_max(peak[:], logits[:], AX.X).then_inc(sm_step, 1)
            dve.wait_ge(sm_step, 1)
            nc.vector.tensor_scalar(logits[:], logits[:], peak[:], None, ALU.subtract).then_inc(peak_ready, 1)
            dve.wait_ge(exp_ready, 1)
            nc.vector.reduce_sum(total[:], expo[:], AX.X).then_inc(sm_step, 1)
            dve.wait_ge(sm_step, 2)
            nc.vector.reciprocal(inverse[:], total[:]).then_inc(sm_step, 1)
            dve.wait_ge(sm_step, 3)
            nc.vector.tensor_scalar(att[:], expo[:], inverse[:], None, ALU.mult).then_inc(att_ready, 1)

            def pair(i):
                split_a(i, 0)
                chunk(i - 1, 1)
                split_a(i, 1)
                chunk(i, 0)

            chunk(0, 0)
            pair(1)
            with dve.Fori(2, DC // 2) as i:
                pair(i)
            chunk(DC // 2 - 1, 1)


def layer0_block(nc, w_hi, w_lo, x, cond_w, bias_k, att_d, weff_d, bias, u_d, x1_d):
    with ExitStack() as ctx:
        def sb(name, shape, dt=F32):
            return ctx.enter_context(nc.sbuf_tensor(name, shape, dt))

        def sem(name):
            return ctx.enter_context(nc.semaphore(name))

        def per_half(name):
            return [sem(f"{name}_{half}") for half in range(2)]

        u_hi = [sb(f"u_hi{j}", [P, L], F32R) for j in range(2)]
        u_lo = [sb(f"u_lo{j}", [P, L], F32R) for j in range(2)]
        x_s = [sb(f"x_s{j}", [P, L]) for j in range(2)]
        u_s = sb("u_s", [P, L])
        x1_s = [sb(f"x1_s{j}", [P, S, HALF // S]) for j in range(2)]
        bias_s = sb("bias_s", [P, HALF])
        kern = sb("kern", [P, K, 2 * P])
        att_s = sb("att_s", [P, NB * K])
        agg = [sb(f"agg{j}", [P, 2 * P]) for j in range(2)]
        ps_u = ctx.enter_context(nc.psum_tensor("ps_u", [P, DC, P], F32))
        ps_g = ctx.enter_context(nc.psum_tensor("ps_g", [P, 2, HALF], F32))
        u_in_s = [u_s[:], x_s[1][:]]
        x_in_s = [x_s[0][:, 0:HALF], x_s[0][:, HALF:L]]
        kern_flat = kern[:].rearrange("p k n -> p (k n)")
        stages = [kern_flat[:, 0:HALF], kern_flat[:, HALF:L], x_s[1][:, 0:HALF], x_s[1][:, HALF:L]]
        WIDE = 12

        def stage(dc):
            return dc % 4 if dc < WIDE else dc % 2

        def before(dc):
            return max([c + 1 for c in range(dc) if stage(c) == stage(dc)], default=0)

        const_in, bias_in = sem("const_in"), per_half("bias_in")
        w_in = [sem(f"w_in{j}") for j in range(4)]
        whi_ready, wlo_ready, w_free = sem("whi2_ready"), sem("wlo2_ready"), sem("w_free")
        x_in = [[sem(f"x_in{half}{j}") for j in range(2)] for half in range(2)]
        u_in = [sem(f"u_in{j}") for j in range(2)]
        u_out, agg_step, u_mm, u_ready = sem("u_out"), sem("agg_step"), sem("u_mm"), sem("u_ready")
        uhi_ready, ulo_ready, gemm = per_half("uhi_ready"), per_half("ulo_ready"), per_half("gemm")
        xb_ready, x1_ready = per_half("xb_ready"), per_half("x1_ready")
        x1_out = [[sem(f"x1_out{half}{j}") for j in range(2)] for half in range(2)]
        block = ctx.enter_context(nc.Block())
        PAIRS = NB // 2

        @block.sync
        def _(sp):
            def load_bias(half):
                sp.dma_start(bias_s[:], bias.rearrange("(a n) -> a n", a=1)[:, half * HALF:(half + 1) * HALF]
                             .to_broadcast([P, HALF])).then_inc(bias_in[half], 16)

            def load_x(i, j):
                n = 2 * i + j
                wait(sp, xb_ready[0], n - 1)
                wait(sp, u_mm, n - 1)
                sp.dma_start(x_s[j][:], x[n, :, :]).then_inc(x_in[0][j], 16)

            def load_x_again(i, j):
                wait(sp, xb_ready[1], 2 * i + j - 1)
                sp.dma_start(x_in_s[j], x[2 * i + j, :, HALF:L]).then_inc(x_in[1][j], 16)

            def load_u(i, j):
                n = 2 * i + j
                wait(sp, uhi_ready[1], n - 1)
                wait(sp, ulo_ready[1], n - 1)
                sp.dma_start(u_in_s[j], u_d[n, :, :]).then_inc(u_in[j], 16)

            def load_w(dc):
                s = stage(dc)
                wait(sp, whi_ready, before(dc))
                wait(sp, wlo_ready, before(dc))
                sp.dma_start(stages[s], weff_d[dc * P:(dc + 1) * P, :]).then_inc(w_in[s], 16)

            load_x(0, 0)
            sp.dma_start(att_s[:], att_d.rearrange("b k -> (b k)").rearrange("(a n) -> a n", a=1)
                         .to_broadcast([P, NB * K])).then_inc(const_in, 16)
            sp.dma_start(kern[:, :, 0:P], cond_w).then_inc(const_in, 16)
            sp.dma_start(kern[:, :, P:2 * P],
                         bias_k.rearrange("(a k) o -> a k o", a=1).to_broadcast([P, K, P])).then_inc(const_in, 16)
            load_x(0, 1)
            load_bias(0)
            with sp.Fori(1, PAIRS) as i:
                for j in range(2):
                    load_x(i, j)
            sp.wait_ge(agg_step, K * NB)
            load_w(0)
            load_w(1)
            sp.wait_ge(u_mm, NB - 1)
            sp.wait_ge(xb_ready[0], NB - 1)
            load_x_again(0, 0)
            sp.wait_ge(u_mm, NB)
            sp.wait_ge(xb_ready[0], NB)
            sp.wait_ge(uhi_ready[0], NB)
            sp.wait_ge(ulo_ready[0], NB)
            sp.wait_ge(u_out, 16 * NB)
            load_u(0, 0)
            load_bias(1)
            for dc in range(2, DC):
                load_w(dc)
                if dc == WIDE + 1:
                    sp.wait_ge(whi_ready, WIDE)
                    sp.wait_ge(wlo_ready, WIDE)
                    load_u(0, 1)
                    load_x_again(0, 1)
            with sp.Fori(1, PAIRS) as i:
                for j in range(2):
                    load_u(i, j)
                    load_x_again(i, j)

        @block.gpsimd
        def _(pool):
            def residual(half, i, j):
                n = 2 * i + j
                pool.wait_ge(x_in[half][j], 16 * i + 16)
                wait(pool, x1_out[half][j], 16 * i)
                src = x_s[j][:, 0:HALF] if half == 0 else x_in_s[j]
                nc.gpsimd.tensor_tensor(x1_s[j][:].rearrange("p s q -> p q s"),
                                        src.rearrange("p (q s) -> p q s", s=S),
                                        bias_s[:].rearrange("p (q s) -> p q s", s=S), ALU.add).then_inc(xb_ready[half], 1)

            for half in range(2):
                pool.wait_ge(bias_in[half], 16)
                for j in range(2):
                    if half == 1:
                        pool.wait_ge(x1_out[0][j], 16 * PAIRS)
                    residual(half, 0, j)
                with pool.Fori(1, PAIRS) as i:
                    residual(half, i, 0)
                    residual(half, i, 1)

        @block.tensor
        def _(pe):
            def make_u(i, j):
                n = 2 * i + j
                pe.wait_ge(x_in[0][j], 16 * i + 16)
                pe.wait_ge(agg_step, K * (n + 1))
                wait(pe, u_ready, n)
                for dc in range(DC):
                    mm = nc.tensor.matmul(ps_u[:, dc, :], x_s[j][:, dc * P:(dc + 1) * P], agg[j][:, 0:P],
                                          start=True, stop=True)
                mm.then_inc(u_mm, 1)

            def products(half, i, j, following=None, opening=False, closing=False):
                n = 2 * i + j
                pe.wait_ge(uhi_ready[half], n + 1)
                pe.wait_ge(ulo_ready[half], n + 1)
                wait(pe, x1_ready[half], n - 1)
                if half == 1 and isinstance(n, int) and n < 2:
                    pe.wait_ge(x1_ready[0], NB - 1 + n)
                for dc in range(DC):
                    if opening:
                        pe.wait_ge(whi_ready, dc + 1)
                        pe.wait_ge(wlo_ready, dc + 1)
                    for u, w in ((u_hi, w_hi), (u_hi, w_lo), (u_lo, w_hi)):
                        for c in range(2):
                            mm = nc.tensor.matmul(ps_g[:, j, c * 512:(c + 1) * 512], u[j][:, dc * P:(dc + 1) * P],
                                                  w[:, dc, c * 512:(c + 1) * 512],
                                                  start=(dc == 0 and u is u_hi and w is w_hi),
                                                  stop=(dc == DC - 1 and u is u_lo))
                    if closing and dc < DC - 1:
                        mm.then_inc(w_free, 1)
                    if dc == DC // 2 - 1 and following is not None:
                        make_u(*following)
                mm.then_inc(gemm[half], 1)

            make_u(0, 0)
            products(0, 0, 0, (0, 1))
            products(0, 0, 1, (1, 0))
            with pe.Fori(1, PAIRS - 1) as i:
                products(0, i, 0, (i, 1))
                products(0, i, 1, (i + 1, 0))
            products(0, PAIRS - 1, 0, (PAIRS - 1, 1))
            products(0, PAIRS - 1, 1, closing=True)
            products(1, 0, 0, opening=True)
            products(1, 0, 1)
            with pe.Fori(1, PAIRS) as i:
                products(1, i, 0)
                products(1, i, 1)

        def w_replaceable(eng, dc):
            if dc < DC - 1:
                eng.wait_ge(w_free, dc + 1)
            else:
                eng.wait_ge(gemm[0], NB)

        @block.scalar
        def _(act):
            def split_u(half, i, j):
                n = 2 * i + j
                if half == 0:
                    act.wait_ge(u_ready, n + 1)
                    act.dma_start(u_d[n, :, :], u_s[:]).then_inc(u_out, 16)
                else:
                    act.wait_ge(u_in[j], 16 * i + 16)
                    if isinstance(n, int) and n < 2:
                        act.wait_ge(gemm[0], NB - 1 + n)
                wait(act, gemm[half], n - 1)
                nc.scalar.activation(u_hi[j][:], u_s[:] if half == 0 else u_in_s[j], ACT.Copy).then_inc(uhi_ready[half], 1)

            def store(half, i, j):
                n = 2 * i + j
                act.wait_ge(x1_ready[half], n + 1)
                act.dma_start(x1_d[n, :, :, half * HALF // S:(half + 1) * HALF // S],
                              x1_s[j][:]).then_inc(x1_out[half][j], 16)

            split_u(0, 0, 0)
            split_u(0, 0, 1)
            store(0, 0, 0)
            with act.Fori(1, PAIRS) as i:
                split_u(0, i, 0)
                store(0, i - 1, 1)
                split_u(0, i, 1)
                store(0, i, 0)
            split_u(1, 0, 0)
            for dc in range(DC):
                s = stage(dc)
                act.wait_ge(w_in[s], 16 * sum(1 for c in range(dc + 1) if stage(c) == s))
                w_replaceable(act, dc)
                nc.scalar.activation(w_hi[:, dc, :], stages[s], ACT.Copy).then_inc(whi_ready, 1)
            split_u(1, 0, 1)
            store(0, PAIRS - 1, 1)
            store(1, 0, 0)
            with act.Fori(1, PAIRS) as i:
                split_u(1, i, 0)
                store(1, i - 1, 1)
                split_u(1, i, 1)
                store(1, i, 0)
            store(1, PAIRS - 1, 1)
            act.wait_ge(x1_out[1][0], 16 * PAIRS)
            act.wait_ge(x1_out[1][1], 16 * PAIRS)

        @block.vector
        def _(dve):
            def aggregate(i, j):
                n = 2 * i + j
                wait(dve, u_mm, n - 1)
                for k in range(K):
                    w = att_s[:, bass.ds(K * n + k, 1)]
                    if k == 0:
                        op = nc.vector.tensor_scalar(agg[j][:], kern[:, 0, :], w, None, ALU.mult)
                    else:
                        dve.wait_ge(agg_step, K * n + k)
                        op = nc.vector.scalar_tensor_tensor(out=agg[j][:], in0=kern[:, k, :], scalar=w,
                                                            in1=agg[j][:], op0=ALU.mult, op1=ALU.add)
                    op.then_inc(agg_step, 1)

            def take_u(half, i, j):
                n = 2 * i + j
                if half == 0:
                    dve.wait_ge(u_mm, n + 1)
                    dve.wait_ge(agg_step, K * (n + 1))
                    wait(dve, uhi_ready[0], n)
                    wait(dve, ulo_ready[0], n)
                    wait(dve, u_out, 16 * n)
                    nc.vector.tensor_tensor(u_s[:].rearrange("p (c o) -> p c o", c=DC), ps_u[:],
                                            agg[j][:, P:2 * P].unsqueeze(1).to_broadcast([P, DC, P]),
                                            ALU.add).then_inc(u_ready, 1)
                dve.wait_ge(uhi_ready[half], n + 1)
                wait(dve, gemm[half], n - 1)
                nc.vector.tensor_tensor(u_lo[j][:], u_s[:] if half == 0 else u_in_s[j], fp32(u_hi[j][:]),
                                        ALU.subtract).then_inc(ulo_ready[half], 1)

            def take_x1(half, i, j):
                n = 2 * i + j
                dve.wait_ge(gemm[half], n + 1)
                dve.wait_ge(xb_ready[half], n + 1)
                x1 = x1_s[j][:].rearrange("p s q -> p q s")
                nc.vector.tensor_tensor(x1, ps_g[:, j, :].rearrange("p (q s) -> p q s", s=S), x1,
                                        ALU.add).then_inc(x1_ready[half], 1)

            dve.wait_ge(const_in, 48)
            aggregate(0, 0)
            take_u(0, 0, 0)
            aggregate(0, 1)
            take_u(0, 0, 1)
            aggregate(1, 0)
            take_x1(0, 0, 0)
            with dve.Fori(1, PAIRS - 1) as i:
                take_u(0, i, 0)
                aggregate(i, 1)
                take_x1(0, i - 1, 1)
                take_u(0, i, 1)
                aggregate(i + 1, 0)
                take_x1(0, i, 0)
            take_u(0, PAIRS - 1, 0)
            aggregate(PAIRS - 1, 1)
            take_x1(0, PAIRS - 2, 1)
            take_u(0, PAIRS - 1, 1)
            take_x1(0, PAIRS - 1, 0)
            take_u(1, 0, 0)
            for dc in range(DC):
                dve.wait_ge(whi_ready, dc + 1)
                w_replaceable(dve, dc)
                nc.vector.tensor_tensor(w_lo[:, dc, :], stages[stage(dc)], fp32(w_hi[:, dc, :]),
                                        ALU.subtract).then_inc(wlo_ready, 1)
            take_u(1, 0, 1)
            take_x1(0, PAIRS - 1, 1)
            take_x1(1, 0, 0)
            with dve.Fori(1, PAIRS) as i:
                take_u(1, i, 0)
                take_x1(1, i - 1, 1)
                take_u(1, i, 1)
                take_x1(1, i, 0)
            take_x1(1, PAIRS - 1, 1)


def layer1_block(nc, x1_d, cond_t, conv_w, ctx_w, fside, up, down, perm, ident, z_d, y_d, out):
    with ExitStack() as ctx:
        def sb(name, shape, dt=F32):
            return ctx.enter_context(nc.sbuf_tensor(name, shape, dt))

        def sem(name):
            return ctx.enter_context(nc.semaphore(name))

        def bank(name, n=1):
            return ctx.enter_context(nc.psum_tensor(name, [P, n, 512], F32))

        up_hi, up_lo = sb("up_hi", [P, H, M], F32R), sb("up_lo", [P, H, M], F32R)
        dn_hi, dn_lo = sb("dn_hi", [P, H, MC * P], F32R), sb("dn_lo", [P, H, MC * P], F32R)
        cw_hi, cw_lo = sb("cw_hi", [P, G * 3, P], F32R), sb("cw_lo", [P, G * 3, P], F32R)
        xp = [sb(f"xp{j}", [P, Q + 2]) for j in range(2)]
        xp_hi, xp_lo = sb("xp_hi", [P, Q + 2], F32R), sb("xp_lo", [P, Q + 2], F32R)
        z_s = sb("z_s", [P, Q])
        zt_s = sb("zt_s", [P, 4, S, C])
        t_s = [sb(f"t_s{j}", [P, RB]) for j in range(2)]
        t_hi, t_lo = sb("t_hi", [P, RB], F32R), sb("t_lo", [P, RB], F32R)
        g_s = sb("g_s", [P, MC, RB])
        g_hi, g_lo = sb("g_hi", [P, MC, RB], F32R), sb("g_lo", [P, MC, RB], F32R)
        y_s = [sb(f"y_s{j}", [P, RB]) for j in range(2)]
        yt_s = [sb(f"yt_s{j}", [P, 4, C]) for j in range(2)]
        x1_s = [sb(f"x1f_s{j}", [P, S, P]) for j in range(2)]
        o_s = [sb(f"o_s{j}", [P, 512]) for j in range(2)]
        idx = sb("idx", [P, H], I32)
        id_s = sb("id_s", [P, P])
        cbias = sb("cbias", [P, G, NB])
        fs_s = sb("fs_s", [P, G])

        ps_up = bank("ps_up", MC)
        ps_c, ps_zt, ps_y, ps_f = bank("ps_c"), bank("ps_zt"), bank("ps_y"), bank("ps_f")

        ctx_in = sem("ctx_in")
        small_in, cw_in, cw_zero, w_in = sem("small_in"), sem("cw_in"), sem("cw_zero"), [sem(f"l1w_in{j}") for j in range(2)]
        pad_ready, ctx_mm, cbias_ready = sem("pad_ready"), sem("ctx_mm"), sem("cbias_ready")
        wsplit_hi, wsplit_lo = sem("wsplit_hi"), sem("wsplit_lo")
        xp_in = [sem(f"xp_in{j}") for j in range(2)]
        xhi_ready, xlo_ready, conv_done, z_ready, zt_done, zt_ready, z_out = (sem(n) for n in (
            "xhi_ready", "xlo_ready", "conv_done", "z_ready", "zt_done", "zt_ready", "z_out"))
        t_in = [sem(f"t_in{j}") for j in range(2)]
        thi_ready, tlo_ready, up_done, gelu_done, ghi_ready, glo_ready, down_done, y_ready = (sem(n) for n in (
            "thi_ready", "tlo_ready", "up_done", "gelu_done", "ghi_ready", "glo_ready", "down_done", "y_ready"))
        gather_clear, scatter_clear = sem("gather_clear"), sem("scatter_clear")
        block_scattered, block_gathered = sem("block_scattered"), sem("block_gathered")
        y_out = [sem(f"y_out{j}") for j in range(2)]
        yt_in = [sem(f"yt_in{j}") for j in range(2)]
        x1_in = [sem(f"x1f_in{j}") for j in range(2)]
        fin_done, o_ready = sem("fin_done"), sem("o_ready")
        o_out = [sem(f"o_out{j}") for j in range(2)]
        block = ctx.enter_context(nc.Block())

        STEPS = BLOCKS * H
        CW = G * 3 * P
        g_flat = g_s[:].rearrange("p c n -> p (c n)")
        stage = [g_flat[:, 0:2 * M], g_flat[:, 2 * M:4 * M]]
        cw_stage = g_flat[:, 0:CW]
        xp_pair = [(xp_hi[:], xp_lo[:]), (g_hi[:].rearrange("p c n -> p (c n)")[:, 0:Q + 2],
                                          g_lo[:].rearrange("p c n -> p (c n)")[:, 0:Q + 2])]
        ps_conv = [ps_c[:, 0, :], ps_up[:, 0, :]]
        z_pair = [z_s[:], y_s[0][:]]
        chunks = []
        for h in range(0, H, 2):
            chunks.append((up_hi[:, h:h + 2, :], up_lo[:, h:h + 2, :], up[:, h:h + 2, :]))
            chunks.append((dn_hi[:, h:h + 2, :], dn_lo[:, h:h + 2, :], down[:, h:h + 2, :]))

        def exists(k, h, offset):
            return not isinstance(k, int) or 0 <= H * k + h + offset < STEPS

        def drive(eng, step):
            for h in range(2 * H - LEAD, H):
                step(-2, h, 0)
            for k in (-1, 0, 1):
                for h in range(H):
                    step(k, h, k % 2)
            with eng.Fori(1, BLOCKS // 2 - 1) as i:
                for parity in range(2):
                    for h in range(H):
                        step(2 * i + parity, h, parity)
            for k in (BLOCKS - 2, BLOCKS - 1, BLOCKS):
                for h in range(H):
                    step(k, h, k % 2)
            step(BLOCKS + 1, 0, 1)
            step(BLOCKS + 1, 1, 1)

        def lead(k):
            return isinstance(k, int) and k < 0

        def chunk_of(k, h):
            n = H * k + h + LEAD
            return n if n < len(chunks) else None

        def pair_of(k, h):
            return h % 2 if isinstance(k, int) and k < 0 else 0

        def paired(k, h):
            return isinstance(k, int) and (k < 0 or (k == 0 and h == 0))

        def t_pair(k, h):
            if late(k, h) and h % 2 == 1:
                return xp_hi[:, 0:RB], xp_lo[:, 0:RB]
            return t_hi[:], t_lo[:]

        def late(k, h):
            return isinstance(k, int) and H * k + h > STEPS - LEAD

        def early(k, h):
            return isinstance(k, int) and H * k + h > STEPS - LEAD + 1

        def t_users(k, h):
            s = H * k + h
            return MC * (s - 1 if late(k, h) else s)

        def conv_unit(k, h):
            return H * k + h + LEAD, h % 2, SB * k + (h + LEAD) // G, h % G

        def final_unit(k, h):
            return H * (k - 1) + h, h % 2, SB * (k - 1) + h // 4, h % 4

        def before(k, h, n=1):
            return (k, h - n) if h >= n else (k - 1, h - n + H)

        def after(k, h):
            return (k, h + 1) if h < H - 1 else (k + 1, 0)

        @block.sync
        def _(sp):
            sp.dma_start(id_s[:], ident).then_inc(small_in, 16)
            sp.dma_start(idx[:], perm).then_inc(small_in, 16)
            sp.wait_ge(cw_zero, 1)
            for s in range(S):
                for tau in (-1, 0, 1):
                    lo, hi = max(0, 4 * tau + s - 4), min(S - 1, 4 * tau + s + 4)
                    kr = 4 - 4 * tau - s + lo
                    n = hi - lo + 1
                    dst = cw_stage[s * GC:(s + 1) * GC, :].rearrange("p (g m) -> p g m", g=G)
                    off = (tau + 1) * P + lo * GC
                    sp.dma_start(dst[:, :, off:off + n * GC], conv_w[:, :, kr * GC:(kr + n) * GC]).then_inc(cw_in, 16)
            def load_x1(k, h):
                u, j, b, g = conv_unit(k, h)
                wait(sp, xlo_ready, u - 1)
                for s in range(S):
                    sp.dma_start(xp[j][s * GC:(s + 1) * GC, 1:Q + 1],
                                 x1_d[b, g * GC:(g + 1) * GC, s, :]).then_inc(xp_in[j], 16)

            def load_final(k, h, parity):
                v, j, b, c = final_unit(k, h)
                if h == 0:
                    scattered = 16 * (H // 2) * k
                    if not isinstance(k, int):
                        scattered = sp.snap(scattered)
                    wait(sp, y_out[0], scattered)
                    wait(sp, y_out[1], scattered)
                    sp.sem_inc(block_scattered, 1)
                wait(sp, fin_done, v - 1)
                sp.dma_start(yt_s[j][:], y_d[1 - parity][c * 512:(c + 1) * 512, h // 4 * C:(h // 4 + 1) * C]
                             .rearrange("(l p) r -> p l r", p=P)).then_inc(yt_in[j], 16)
                wait(sp, o_ready, v - 1)
                sp.dma_start(x1_s[j][:], x1_d[b, :, :, c * P:(c + 1) * P]).then_inc(x1_in[j], 16)

            def store_out(k, h):
                v, j, b, c = final_unit(k, h)
                sp.wait_ge(o_ready, v + 1)
                sp.dma_start(out[b, :, c * 512:(c + 1) * 512], o_s[j][:]).then_inc(o_out[j], 16)

            def store_z(k, h, parity):
                u = conv_unit(k, h)[0] - 2
                jb = (h + LEAD - 2) // G % SB
                ahead = (h + LEAD - 2) // G // SB
                if jb == 0:
                    wait(sp, tlo_ready, H * (k + ahead - 1))
                    sp.sem_inc(block_gathered, 1)
                sp.wait_ge(zt_ready, u + 1)
                for w in range(4):
                    sp.dma_start(z_d[(parity + ahead) % 2][w * 512:(w + 1) * 512, jb * C:(jb + 1) * C]
                                 .rearrange("(q r) n -> q r n", r=S), zt_s[:, w, :, :]).then_inc(z_out, 16)

            def step(k, h, parity):
                if exists(k, h, LEAD - 2) and (h + LEAD - 2) % G == G - 1:
                    store_z(k, h, parity)
                if exists(k, h, LEAD + 2):
                    load_x1(*after(*after(k, h)))
                if exists(k, h, -H):
                    load_final(k, h, parity)
                if exists(k, h, -H - 2):
                    store_out(*before(k, h, 2))

            sp.wait_ge(pad_ready, 2)
            load_x1(-2, 2 * H - LEAD)
            load_x1(-2, 2 * H - LEAD + 1)
            drive(sp, step)
            sp.wait_ge(o_out[0], 16 * (STEPS // 2))
            sp.wait_ge(o_out[1], 16 * (STEPS // 2))

        @block.gpsimd
        def _(pool):
            nc.gpsimd.memset(cw_stage, 0.0).then_inc(cw_zero, 1)
            nc.gpsimd.memset(xp[0][:], 0.0).then_inc(pad_ready, 1)
            nc.gpsimd.memset(xp[1][:], 0.0).then_inc(pad_ready, 1)

            def gather(k, h, parity):
                s, j = H * k + h, h % 2
                if h == 0:
                    pool.wait_ge(z_out, 64 * SB * (k + 1))
                wait(pool, tlo_ready, s - 1)
                pool.sem_inc(gather_clear, 1)
                nc.gpsimd.indirect_dma_start(
                    out=t_s[j][:], out_offset=None, in_=z_d[parity],
                    in_offset=bass.IndirectOffsetOnAxis(ap=idx[:, h:h + 1], axis=0)).then_inc(t_in[j], 16)

            def load_weights(n):
                if n < len(chunks):
                    pool.wait_ge(wsplit_lo, max(n, 1))
                    pool.dma_start(stage[n % 2].rearrange("p (a b) -> p a b", a=2), chunks[n][2]).then_inc(w_in[n % 2], 16)

            load_weights(0)

            def step(k, h, parity):
                if isinstance(k, int) and k < 0:
                    load_weights(H * k + h + LEAD + 1)
                if exists(k, h, 2):
                    if isinstance(k, int) and H * k + h == -2:
                        pool.wait_ge(small_in, 32)
                        pool.wait_ge(cbias_ready, 1)
                    if h < H - 2:
                        gather(k, h + 2, parity)
                    else:
                        gather(k + 1, h + 2 - H, 1 - parity)
                if exists(k, h, 0):
                    s, j = H * k + h, h % 2
                    pool.wait_ge(y_ready, s + 1)
                    if h == 0:
                        wait(pool, yt_in[0], 16 * (H // 2) * (k - 1))
                        wait(pool, yt_in[1], 16 * (H // 2) * (k - 1))
                    pool.sem_inc(scatter_clear, 1)
                    nc.gpsimd.indirect_dma_start(
                        out=y_d[parity], out_offset=bass.IndirectOffsetOnAxis(ap=idx[:, h:h + 1], axis=0),
                        in_=y_s[j][:], in_offset=None).then_inc(y_out[j], 16)

            drive(pool, step)
            pool.wait_ge(y_out[0], 16 * (STEPS // 2))
            pool.wait_ge(y_out[1], 16 * (STEPS // 2))

        @block.tensor
        def _(pe):
            pe.wait_ge(ctx_in, 96)
            for g in range(G):
                for r in range(S):
                    mm = nc.tensor.matmul(ps_c[r * GC:(r + 1) * GC, 0, g * NB:(g + 1) * NB],
                                          t_s[0][:, g * GC:(g + 1) * GC], t_s[1][:, 0:NB], start=True, stop=True)
            mm.then_inc(ctx_mm, 1)

            def up_part(k, h, mc):
                s = H * k + h
                if mc == 0:
                    pe.wait_ge(tlo_ready, s + 1)
                wait(pe, gelu_done, MC * (s - 1) + mc + 1)
                hi, lo = t_pair(k, h)
                for n, (w, t) in enumerate(((up_hi, hi), (up_hi, lo), (up_lo, hi))):
                    mm = nc.tensor.matmul(ps_up[:, mc, :], w[:, h, mc * P:(mc + 1) * P], t,
                                          start=(n == 0), stop=(n == 2))
                mm.then_inc(up_done, 1)

            def down_part(k, h, mc):
                s = H * k + h
                pe.wait_ge(glo_ready, MC * s + mc + 1)
                if mc == 0:
                    wait(pe, y_ready, s)
                for w, g in ((dn_hi, g_hi), (dn_hi, g_lo), (dn_lo, g_hi)):
                    mm = nc.tensor.matmul(ps_y[:, 0, :], w[:, h, mc * P:(mc + 1) * P], g[:, mc, :],
                                          start=(mc == 0 and w is dn_hi and g is g_hi),
                                          stop=(mc == MC - 1 and w is dn_lo))
                mm.then_inc(down_done, 1)

            def conv(k, h):
                u, j, b, g = conv_unit(k, h)
                pe.wait_ge(xlo_ready, u + 1)
                wait(pe, z_ready, u - 1 if paired(k, h) else u)
                hi, lo = xp_pair[pair_of(k, h)]
                acc = ps_conv[pair_of(k, h)]
                for tau in range(3):
                    for n, (w, x) in enumerate(((cw_hi, hi), (cw_hi, lo), (cw_lo, hi))):
                        mm = nc.tensor.matmul(acc, w[:, 3 * g + tau, :], x[:, tau:tau + Q],
                                              start=(tau == 0 and n == 0), stop=(tau == 2 and n == 2))
                mm.then_inc(conv_done, 1)

            def turn_z(k, h):
                u, _, _, _ = conv_unit(k, h)
                z = z_pair[pair_of(k, h)]
                pe.wait_ge(z_ready, u + 1)
                wait(pe, zt_ready, u)
                for w in range(4):
                    mm = nc.tensor.transpose(ps_zt[:, 0, w * P:(w + 1) * P], z[:, w * P:(w + 1) * P], id_s[:])
                mm.then_inc(zt_done, 1)

            def turn_y(k, h):
                v, j, _, _ = final_unit(k, h)
                pe.wait_ge(yt_in[j], 16 * (H // 2 * (k - 1) + h // 2 + 1))
                wait(pe, o_ready, v)
                for l in range(4):
                    mm = nc.tensor.transpose(ps_f[:, 0, l * P:(l + 1) * P], yt_s[j][:, l, :], id_s[:])
                mm.then_inc(fin_done, 1)

            pe.wait_ge(small_in, 32)
            pe.wait_ge(cbias_ready, 1)
            pe.wait_ge(wsplit_lo, 1)

            def step(k, h, parity):
                if exists(k, h, LEAD):
                    conv(k, h)
                if exists(k, h, LEAD - 1):
                    turn_z(*before(k, h))
                if exists(k, h, -H - 1):
                    turn_y(*before(k, h))
                if isinstance(k, int) and H * k + h == -1:
                    pe.wait_ge(wsplit_lo, 1 + len(chunks))
                    pe.wait_ge(z_ready, LEAD)
                for mc in range(MC):
                    if exists(k, h, 0):
                        down_part(k, h, mc)
                    if exists(k, h, 1):
                        up_part(*after(k, h), mc)

            drive(pe, step)

        @block.scalar
        def _(act):
            act.dma_start(t_s[0][:, 0:C], ctx_w).then_inc(ctx_in, 16)
            act.dma_start(t_s[1][:, 0:NB], cond_t).then_inc(ctx_in, 16)
            for r in range(S):
                act.dma_start(fs_s[r * GC:(r + 1) * GC, :], fside, allow_slow_non_contiguous=True).then_inc(ctx_in, 16)
            act.wait_ge(cw_in, 16 * 12)
            nc.scalar.activation(cw_hi[:].rearrange("p a b -> p (a b)"), cw_stage, ACT.Copy).then_inc(wsplit_hi, 1)

            def split_weights(n):
                act.wait_ge(w_in[n % 2], 16 * (n // 2 + 1))
                nc.scalar.activation(chunks[n][0], stage[n % 2].rearrange("p (a b) -> p a b", a=2),
                                     ACT.Copy).then_inc(wsplit_hi, 1)

            def split_x(k, h):
                u, j, _, _ = conv_unit(k, h)
                act.wait_ge(xp_in[j], 64 * (H // 2 * k + (h + LEAD) // 2 + 1))
                wait(act, conv_done, u - 1 if paired(k, h) else u)
                nc.scalar.activation(xp_pair[pair_of(k, h)][0], xp[j][:], ACT.Copy).then_inc(xhi_ready, 1)

            def split_t(k, h):
                s, j = H * k + h, h % 2
                act.wait_ge(t_in[j], 16 * (H // 2 * k + h // 2 + 1))
                wait(act, up_done, t_users(k, h))
                if isinstance(k, int) and s == STEPS - LEAD + 1:
                    act.wait_ge(conv_done, STEPS)
                nc.scalar.activation(t_pair(k, h)[0], t_s[j][:], ACT.Copy).then_inc(thi_ready, 1)

            act.wait_ge(pad_ready, 2)
            act.wait_ge(cbias_ready, 1)
            split_x(-2, 2 * H - LEAD)

            def gelu(k, h, mc):
                s = H * k + h
                act.wait_ge(up_done, MC * s + mc + 1)
                wait(act, glo_ready, MC * (s - 1) + mc + 1)
                nc.scalar.activation(g_s[:, mc, :], ps_up[:, mc, :], ACT.Gelu).then_inc(gelu_done, 1)

            def step(k, h, parity):
                if not lead(k) and exists(k, h, 1) and not early(*after(k, h)):
                    split_t(*after(k, h))
                if lead(k):
                    split_x(*after(k, h))
                    if chunk_of(k, h) is not None:
                        split_weights(chunk_of(k, h))
                if exists(k, h, LEAD):
                    u, j, b, g = conv_unit(k, h)
                    act.wait_ge(conv_done, u + 1)
                    wait(act, zt_done, u - 1 if paired(k, h) else u)
                    nc.scalar.activation(z_pair[pair_of(k, h)], ps_conv[pair_of(k, h)], ACT.Identity,
                                         bias=cbias[:, g, bass.ds(b, 1)]).then_inc(z_ready, 1)
                    if not lead(k) and exists(k, h, LEAD + 1):
                        split_x(*after(k, h))
                if isinstance(k, int) and H * k + h == -1:
                    split_t(0, 0)
                    act.wait_ge(wsplit_lo, 1 + len(chunks))
                for mc in range(MC - 1):
                    if exists(k, h, 1):
                        gelu(*after(k, h), mc)
                if exists(k, h, 2) and early(*after(*after(k, h))):
                    split_t(*after(*after(k, h)))
                if exists(k, h, 0):
                    s, j = H * k + h, h % 2
                    act.wait_ge(down_done, MC * (s + 1))
                    wait(act, y_out[j], 16 * (H // 2 * k + h // 2))
                    nc.scalar.activation(y_s[j][:], ps_y[:, 0, :], ACT.Copy).then_inc(y_ready, 1)
                if exists(k, h, 1):
                    gelu(*after(k, h), MC - 1)

            drive(act, step)

        @block.vector
        def _(dve):
            dve.wait_ge(ctx_in, 96)
            dve.wait_ge(ctx_mm, 1)
            nc.vector.tensor_tensor(cbias[:], ps_c[:, 0, 0:G * NB].rearrange("p (g b) -> p g b", g=G),
                                    fs_s[:].unsqueeze(2).to_broadcast([P, G, NB]), ALU.add).then_inc(cbias_ready, 1)
            dve.wait_ge(wsplit_hi, 1)
            nc.vector.tensor_tensor(cw_lo[:].rearrange("p a b -> p (a b)"), cw_stage,
                                    fp32(cw_hi[:].rearrange("p a b -> p (a b)")), ALU.subtract).then_inc(wsplit_lo, 1)

            def split_weights(n):
                hi, lo, _ = chunks[n]
                dve.wait_ge(wsplit_hi, n + 2)
                nc.vector.tensor_tensor(lo, stage[n % 2].rearrange("p (a b) -> p a b", a=2), fp32(hi),
                                        ALU.subtract).then_inc(wsplit_lo, 1)

            def split_x(k, h):
                u, j, _, _ = conv_unit(k, h)
                dve.wait_ge(xhi_ready, u + 1)
                wait(dve, conv_done, u - 1 if paired(k, h) else u)
                hi, lo = xp_pair[pair_of(k, h)]
                nc.vector.tensor_tensor(lo, xp[j][:], fp32(hi), ALU.subtract).then_inc(xlo_ready, 1)

            def split_t(k, h):
                s, j = H * k + h, h % 2
                dve.wait_ge(thi_ready, s + 1)
                wait(dve, up_done, t_users(k, h))
                if isinstance(k, int) and s == STEPS - LEAD + 1:
                    dve.wait_ge(conv_done, STEPS)
                hi, lo = t_pair(k, h)
                nc.vector.tensor_tensor(lo, t_s[j][:], fp32(hi), ALU.subtract).then_inc(tlo_ready, 1)

            def take_z(k, h):
                u, j, b, g = conv_unit(k, h)
                dve.wait_ge(zt_done, u + 1)
                if g == 0:
                    wait(dve, z_out, 64 * b)
                nc.vector.tensor_copy(zt_s[:, :, :, g * GC:(g + 1) * GC],
                                      ps_zt[:, 0, :].rearrange("p (w r o) -> p w r o", w=4, r=S)).then_inc(zt_ready, 1)

            def take_final(k, h):
                v, j, b, c = final_unit(k, h)
                n = H // 2 * (k - 1) + h // 2
                dve.wait_ge(fin_done, v + 1)
                dve.wait_ge(x1_in[j], 16 * (n + 1))
                wait(dve, o_out[j], 16 * n)
                nc.vector.tensor_tensor(o_s[j][:].rearrange("p (q s) -> p q s", s=S),
                                        ps_f[:, 0, :].rearrange("p (q s) -> p q s", s=S),
                                        x1_s[j][:].rearrange("p s q -> p q s"), ALU.add).then_inc(o_ready, 1)

            split_x(-2, 2 * H - LEAD)

            def split_g(k, h, mc):
                s = H * k + h
                dve.wait_ge(gelu_done, MC * s + mc + 1)
                wait(dve, down_done, MC * (s - 1) + mc + 1)
                nc.vector.tensor_copy(g_hi[:, mc, :], g_s[:, mc, :]).then_inc(ghi_ready, 1)
                dve.wait_ge(ghi_ready, MC * s + mc + 1)
                nc.vector.tensor_tensor(g_lo[:, mc, :], g_s[:, mc, :], fp32(g_hi[:, mc, :]),
                                        ALU.subtract).then_inc(glo_ready, 1)

            def step(k, h, parity):
                if not lead(k) and exists(k, h, 1) and not early(*after(k, h)):
                    split_t(*after(k, h))
                if lead(k):
                    split_x(*after(k, h))
                    if chunk_of(k, h) is not None:
                        split_weights(chunk_of(k, h))
                if exists(k, h, LEAD - 1):
                    take_z(*before(k, h))
                if exists(k, h, -H - 1):
                    take_final(*before(k, h))
                if not lead(k) and exists(k, h, LEAD + 1):
                    split_x(*after(k, h))
                if isinstance(k, int) and H * k + h == -1:
                    split_t(0, 0)
                if exists(k, h, 1):
                    for mc in range(MC):
                        split_g(*after(k, h), mc)
                        if mc == MC - 2 and exists(k, h, 2) and early(*after(*after(k, h))):
                            split_t(*after(*after(k, h)))

            drive(dve, step)


def build(nc, x, cond_t, fside, w0, b0, w1, b1, w2, b2, cond_w, bias_k, w_t, bias, lora_a, lora_b, coeffs, scales,
          conv_w, ctx_w, up, down, perm, ident, out):
    def scratch(name, shape):
        return nc.dram_tensor(name, shape, F32, kind="Internal").ap()

    att_d = scratch("att_d", [NB, K])
    weff_d = scratch("weff_d", [L, HALF])
    u_d = scratch("u_d", [NB, P, DC * P])
    x1_d = scratch("x1_d", [NB, C, S, Q])
    z_d = [scratch(f"z_d{j}", [L, RB]) for j in range(2)]
    y_d = [scratch(f"y_d{j}", [L, RB]) for j in range(2)]
    with (nc.sbuf_tensor("w_hi", [P, DC, HALF], F32R) as w_hi, nc.sbuf_tensor("w_lo", [P, DC, HALF], F32R) as w_lo):
        setup_block(nc, w_hi, w_lo, cond_t, w0, b0, w1, b1, w2, b2, w_t, lora_a, lora_b, coeffs, scales, att_d, weff_d)
        layer0_block(nc, w_hi, w_lo, x, cond_w, bias_k, att_d, weff_d, bias, u_d, x1_d)
    layer1_block(nc, x1_d, cond_t, conv_w, ctx_w, fside, up, down, perm, ident, z_d, y_d, out)


def kernel(**inputs):
    import numpy as np
    import concourse.bacc as bacc
    from concourse.bass_utils import run_bass_kernel_spmd

    def v(name):
        return np.asarray(inputs[name])

    def by_partition(a):
        return a.reshape(KC, P).T

    def repeat_rank(a):
        return np.broadcast_to(a[:, None], (16, 16)).reshape(ER)

    arrays = {
        "x": v("x"),
        "cond_t": v("cond_128").T,
        "fside": v("fside_S_0").reshape(G, GC).T,
        "w0": v("L0_cond_W0"), "b0": v("L0_cond_b0"),
        "w1": v("L0_cond_W1"), "b1": v("L0_cond_b1"),
        "w2": v("L0_cond_W2"), "b2": v("L0_cond_b2"),
        "cond_w": v("L0_cond_weight")[..., 0].transpose(2, 0, 1),
        "bias_k": v("L0_cond_bias_k"),
        "w_t": v("L0_ffn_W").T,
        "bias": v("L0_ffn_bias"),
        "lora_a": v("L0_ffn_A").reshape(ER, L),
        "lora_b": v("L0_ffn_Bf").transpose(0, 2, 1).reshape(ER, L),
        "coeffs": by_partition(repeat_rank(v("L0_ffn_coeffs"))),
        "scales": by_partition(repeat_rank(v("L0_ffn_scales"))),
        "conv_w": v("L1_cond_weight").reshape(G, GC, GC, TAPS)[..., ::-1].transpose(2, 0, 3, 1).reshape(GC, G, TAPS * GC),
        "ctx_w": v("L1_cond_c_weight").T,
        "up": v("L1_ffn_up").transpose(1, 0, 2),
        "down": v("L1_ffn_down").reshape(H, MC, P, P).transpose(2, 0, 1, 3).reshape(P, H, MC * P),
        "perm": v("L1_ffn_perm").reshape(H, P).T,
        "ident": np.eye(P, dtype=np.float32),
    }
    nc = bacc.Bacc("TRN2", target_bir_lowering=False, num_devices=1)
    args, feed = [], {}
    for name, a in arrays.items():
        a = np.ascontiguousarray(a)
        feed[f"in_{name}"] = a
        args.append(nc.dram_tensor(f"in_{name}", a.shape, mybir.dt.from_np(a.dtype), kind="ExternalInput").ap())
    out = nc.dram_tensor("out_0_dram", (NB, C, L), F32, kind="ExternalOutput").ap()
    build(nc, *args, out)
    r = run_bass_kernel_spmd(nc, [feed], core_ids=[0])
    return r.results[0]["out_0_dram"]
```

```python
import concourse.bass as bass
from concourse import mybir
from contextlib import ExitStack

F32 = mybir.dt.float32
F32R = mybir.dt.float32r
I32 = mybir.dt.int32
ALU = mybir.AluOpType
ACT = mybir.ActivationFunctionType
AX = mybir.AxisListType

P = 128
NB, C, L = 32, 128, 2048
DC = L // P
HALF = L // 2
K = 8
ER = 256
KC = ER // P
G, GC, TAPS, S = 4, 32, 9, 4
Q = L // S
H, M = 16, 512
MC = M // P
RB = 512
BLOCKS = NB * C // RB
SB = RB // C
LEAD = 20


def wait(eng, sem, value):
    if isinstance(value, int) and value <= 0:
        return
    eng.wait_ge(sem, value)


def fp32(ap):
    return ap.bitcast(F32)


class Shared:

    def __init__(self, nc, ctx):
        def sb(name, shape, dt=F32):
            return ctx.enter_context(nc.sbuf_tensor(name, shape, dt))

        def sem(name):
            return ctx.enter_context(nc.semaphore(name))

        self.kern = sb("kern", [P, L])
        self.u_s = sb("u_s", [P, L + 4])
        self.x1_s = sb("x1_s", [P, 2, HALF])
        self.cbias = sb("cbias", [P, G, NB])
        self.weff_out = [sem(f"weff_out{j}") for j in range(2)]
        self.const_in, self.agg_step, self.u_mm = sem("const_in"), sem("agg_step"), sem("u_mm")
        self.x_in = [[sem(f"x_in{half}{j}") for j in range(2)] for half in range(2)]
        self.x1_out = [[sem(f"x1_out{half}{j}") for j in range(2)] for half in range(2)]
        self.cw_in, self.pad_ready = sem("cw_in"), sem("pad_ready")
        self.xp_in = [sem(f"xp_in{j}") for j in range(4)]
        self.xp = [self.u_s[:, j * (Q + 2):(j + 1) * (Q + 2)] for j in range(3)]
        self.t_s = [self.u_s[:, 2 * (Q + 2) + j * RB:2 * (Q + 2) + (j + 1) * RB] for j in range(2)]

    def add_layer0(self, nc, ctx):
        self.x0 = ctx.enter_context(nc.sbuf_tensor("x0", [P, L], F32))
        self.att_s = ctx.enter_context(nc.sbuf_tensor("att_s", [P, NB * K], F32))
        self.agg = [ctx.enter_context(nc.sbuf_tensor(f"agg{j}", [P, 2 * P], F32)) for j in range(2)]
        self.ps_u = ctx.enter_context(nc.psum_tensor("ps_u", [P, DC, P], F32))
        self.ps_g = ctx.enter_context(nc.psum_tensor("ps_g", [P, 2, HALF], F32))

    def experts(self):
        return self.kern[:].rearrange("p (k n) -> p k n", k=K)

    def load_group(self, eng, x1_d, xp, j, b, g):
        for s in range(S):
            eng.dma_start(xp[s * GC:(s + 1) * GC, 1:Q + 1],
                          x1_d[b, g * GC:(g + 1) * GC, s, :]).then_inc(self.xp_in[j], 16)


def aggregate(nc, dve, sh, n, j):
    kern = sh.experts()
    wait(dve, sh.u_mm, n - 1)
    for k in range(K):
        w = sh.att_s[:, bass.ds(K * n + k, 1)]
        if k == 0:
            op = nc.vector.tensor_scalar(sh.agg[j][:], kern[:, 0, :], w, None, ALU.mult)
        else:
            dve.wait_ge(sh.agg_step, K * n + k)
            op = nc.vector.scalar_tensor_tensor(out=sh.agg[j][:], in0=kern[:, k, :], scalar=w,
                                                in1=sh.agg[j][:], op0=ALU.mult, op1=ALU.add)
        op.then_inc(sh.agg_step, 1)


def u_product(nc, sh, x_s, j):
    for dc in range(DC):
        mm = nc.tensor.matmul(sh.ps_u[:, dc, :], x_s[:, dc * P:(dc + 1) * P], sh.agg[j][:, 0:P],
                              start=True, stop=True)
    mm.then_inc(sh.u_mm, 1)


def setup_block(nc, sh, w_hi, w_lo, x, cond_w, bias_k, cond_t, w0, b0, w1, b1, w2, b2, w_t, lora_a, lora_b, coeffs, scales, att_d, weff_d):
    with ExitStack() as ctx:
        def sb(name, shape, dt=F32):
            return ctx.enter_context(nc.sbuf_tensor(name, shape, dt))

        def sem(name):
            return ctx.enter_context(nc.semaphore(name))

        cond_s = sb("cond_s", [P, NB])
        w0_s, w1_s, w2_s = sb("w0_s", [P, P]), sb("w1_s", [P, P]), sb("w2_s", [P, K])
        b0_s, b1_s, b2_s = sb("b0_s", [P, 1]), sb("b1_s", [P, 1]), sb("b2_s", [NB, K])
        h0, h1 = sb("h0", [P, NB]), sb("h1", [P, NB])
        logits, expo, att = sb("logits", [NB, K]), sb("expo", [NB, K]), sb("att", [NB, K])
        peak, total, inverse = sb("peak", [NB, 1]), sb("total", [NB, 1]), sb("inverse", [NB, 1])
        co_s, sc_s, cs = sb("co_s", [P, KC]), sb("sc_s", [P, KC]), sb("cs", [P, KC])
        b_s = [sh.kern[:], sh.x0[:]]
        b_hi, b_lo = sb("b_hi", [P, KC, L], F32R), sb("b_lo", [P, KC, L], F32R)
        a_s = [sb(f"a_s{j}", [P, KC, P]) for j in range(2)]
        a_hi = [sb(f"a_hi{j}", [P, KC, P], F32R) for j in range(2)]
        a_lo = [sb(f"a_lo{j}", [P, KC, P], F32R) for j in range(2)]
        wt_s = [[sh.u_s[:, 0:HALF], sh.u_s[:, HALF:L]], [sh.x1_s[:, 0, :], sh.x1_s[:, 1, :]]]
        ps_even = sh.ps_u[:].rearrange("p c o -> p (c o)")
        acc = [[ps_even[:, 0:HALF], ps_even[:, HALF:L]], [sh.ps_g[:, 0, :], sh.ps_g[:, 1, :]]]
        ps_h0, ps_h1, ps_lg = acc[1][1][:, 0:NB], acc[1][1][:, P:P + NB], sh.ps_g[0:NB, 1, 512:512 + K]

        cond_in, mlp_in, scale_in = sem("cond_in"), sem("mlp_in"), sem("scale_in")
        b_in = [sem(f"b_in{n}") for n in range(2 * KC)]
        a_in = [sem(f"a_in{j}") for j in range(2)]
        wt_in = [[sem(f"wt_in{j}{half}") for half in range(2)] for j in range(2)]
        h0_mm, h0_ready, h1_mm, h1_ready = sem("h0_mm"), sem("h0_ready"), sem("h1_mm"), sem("h1_ready")
        lg_mm, lg_ready, peak_ready, exp_ready, att_ready = (sem(n) for n in (
            "lg_mm", "lg_ready", "peak_ready", "exp_ready", "att_ready"))
        sm_step, att_out = sem("sm_step"), sem("att_out")
        cs_ready, bsc_ready, bhi_ready, blo_ready = sem("cs_ready"), sem("bsc_ready"), sem("bhi_ready"), sem("blo_ready")
        ahi_ready, alo_ready, whi_ready, wlo_ready = sem("ahi_ready"), sem("alo_ready"), sem("whi_ready"), sem("wlo_ready")
        item_mm = [sem(f"item_mm{half}") for half in range(2)]
        item_sum = [sem(f"item_sum{half}") for half in range(2)]
        weff_out = sh.weff_out
        block = ctx.enter_context(nc.Block())

        a_v = lora_a.rearrange("(c p) d -> p c d", p=P)
        pieces = [(c, slice(half * HALF, (half + 1) * HALF)) for half in range(2) for c in range(KC)]

        @block.sync
        def _(sp):
            def load_a(dc, j):
                wait(sp, alo_ready, dc - 1)
                sp.dma_start(a_s[j][:], a_v[:, :, bass.ds(dc * P, P)]).then_inc(a_in[j], 16)

            def load(i, j):
                dc = 2 * i + j
                if not isinstance(dc, int) or dc < DC - 1:
                    load_a(dc + 1, 1 - j)
                wait(sp, wlo_ready, dc - 1)
                sp.dma_start(wt_s[j][0], w_t[bass.ds(dc * P, P), 0:HALF]).then_inc(wt_in[j][0], 16)
                wait(sp, weff_out[j], 16 * i)
                sp.dma_start(wt_s[j][1], w_t[bass.ds(dc * P, P), HALF:L]).then_inc(wt_in[j][1], 16)

            for n, (c, cols) in enumerate(pieces):
                sp.dma_start(b_s[c][:, cols], lora_b[c * P:(c + 1) * P, cols]).then_inc(b_in[n], 16)
                if n == 0:
                    load_a(0, 0)
                if n == 1:
                    load(0, 0)
            load(0, 1)
            with sp.Fori(1, DC // 2 - 1) as i:
                load(i, 0)
                load(i, 1)
            load(DC // 2 - 1, 0)
            load(DC // 2 - 1, 1)

        @block.tensor
        def _(pe):
            def attention(part):
                if part == 0:
                    pe.wait_ge(cond_in, 2 * 16)
                    nc.tensor.matmul(ps_h0, w0_s[:], cond_s[:], start=True, stop=True).then_inc(h0_mm, 1)
                elif part == 1:
                    pe.wait_ge(mlp_in, 5 * 16)
                    pe.wait_ge(h0_ready, 1)
                    nc.tensor.matmul(ps_h1, w1_s[:], h0[:], start=True, stop=True).then_inc(h1_mm, 1)
                elif part == 2:
                    pe.wait_ge(h1_ready, 1)
                    nc.tensor.matmul(ps_lg, h1[:], w2_s[:], start=True, stop=True).then_inc(lg_mm, 1)

            def chunk(i, j):
                dc = 2 * i + j
                pe.wait_ge(alo_ready, dc + 1)
                for half in range(2):
                    wait(pe, item_sum[half], dc - 1)
                    if isinstance(dc, int) and dc == 1 and half == 1:
                        pe.wait_ge(lg_ready, 1)
                    for kc in range(KC):
                        if isinstance(dc, int) and dc == 0:
                            pe.wait_ge(blo_ready, 2 * half + kc + 1)
                        for w, b in ((a_hi, b_hi), (a_hi, b_lo), (a_lo, b_hi)):
                            for n in range(2):
                                at = half * HALF + n * 512
                                mm = nc.tensor.matmul(acc[j][half][:, n * 512:(n + 1) * 512], w[j][:, kc, :],
                                                      b[:, kc, at:at + 512],
                                                      start=(kc == 0 and w is a_hi and b is b_hi),
                                                      stop=(kc == KC - 1 and w is a_lo))
                    mm.then_inc(item_mm[half], 1)
                    if isinstance(dc, int):
                        attention(2 * dc + half)

            chunk(0, 0)
            chunk(0, 1)
            with pe.Fori(1, DC // 2) as i:
                chunk(i, 0)
                chunk(i, 1)
            pe.wait_ge(item_sum[0], DC - 1)
            pe.wait_ge(item_sum[1], DC - 1)
            pe.wait_ge(sh.x_in[0][0], 16)
            pe.wait_ge(sh.agg_step, K)
            u_product(nc, sh, sh.x0, 0)

        @block.scalar
        def _(act):
            act.dma_start(co_s[:], coeffs).then_inc(scale_in, 16)
            act.dma_start(sc_s[:], scales).then_inc(scale_in, 16)
            act.dma_start(cond_s[:], cond_t).then_inc(cond_in, 16)
            act.dma_start(w0_s[:], w0).then_inc(cond_in, 16)

            def split_b(n):
                c, cols = pieces[n]
                act.wait_ge(bsc_ready, n + 1)
                nc.scalar.activation(b_hi[:, c, cols], b_s[c][:, cols], ACT.Copy).then_inc(bhi_ready, 1)

            def split_a(i, j):
                dc = 2 * i + j
                act.wait_ge(a_in[j], 16 * i + 16)
                wait(act, item_mm[1], dc - 1)
                nc.scalar.activation(a_hi[j][:], a_s[j][:], ACT.Copy).then_inc(ahi_ready, 1)

            def take(i, j):
                dc = 2 * i + j
                act.wait_ge(item_sum[0], dc + 1)
                nc.scalar.activation(w_hi[:, bass.ds(dc, 1), :].rearrange("p a n -> p (a n)"), wt_s[j][0],
                                     ACT.Copy).then_inc(whi_ready, 1)
                act.wait_ge(item_sum[1], dc + 1)
                act.dma_start(weff_d[bass.ds(dc * P, P), :], wt_s[j][1]).then_inc(weff_out[j], 16)

            split_a(0, 0)
            split_b(0)
            split_b(1)
            split_b(2)
            split_b(3)
            act.wait_ge(mlp_in, 5 * 16)
            act.wait_ge(h0_mm, 1)
            nc.scalar.activation(h0[:], ps_h0, ACT.Gelu, bias=b0_s[:]).then_inc(h0_ready, 1)
            split_a(0, 1)
            act.wait_ge(h1_mm, 1)
            nc.scalar.activation(h1[:], ps_h1, ACT.Gelu, bias=b1_s[:]).then_inc(h1_ready, 1)
            take(0, 0)
            act.wait_ge(peak_ready, 1)
            nc.scalar.activation(expo[:], logits[:], ACT.Exp).then_inc(exp_ready, 1)
            act.wait_ge(att_ready, 1)
            act.dma_start(att_d, att[:]).then_inc(att_out, 16)
            act.wait_ge(blo_ready, 2 * KC)
            act.dma_start(sh.x0[:], x[0, :, :]).then_inc(sh.x_in[0][0], 16)

            def pair(i):
                split_a(i, 0)
                take(i - 1, 1)
                split_a(i, 1)
                take(i, 0)

            pair(1)
            with act.Fori(2, DC // 2) as i:
                pair(i)
            take(DC // 2 - 1, 1)

        @block.gpsimd
        def _(pool):
            for dst, src in ((b0_s, b0.rearrange("(p a) -> p a", a=1)), (w1_s, w1), (b1_s, b1.rearrange("(p a) -> p a", a=1)),
                             (w2_s, w2), (b2_s, b2.rearrange("(a k) -> a k", a=1).to_broadcast([NB, K]))):
                pool.dma_start(dst[:], src).then_inc(mlp_in, 16)
            pool.wait_ge(blo_ready, 2 * KC)
            pool.dma_start(sh.experts()[:, :, 0:P], cond_w).then_inc(sh.const_in, 16)
            pool.dma_start(sh.experts()[:, :, P:2 * P],
                           bias_k.rearrange("(a k) o -> a k o", a=1).to_broadcast([P, K, P])).then_inc(sh.const_in, 16)
            pool.wait_ge(att_out, 16)
            pool.dma_start(sh.att_s[:], att_d.rearrange("b k -> (b k)").rearrange("(a n) -> a n", a=1)
                           .to_broadcast([P, NB * K])).then_inc(sh.const_in, 16)

        @block.vector
        def _(dve):
            dve.wait_ge(scale_in, 32)
            nc.vector.tensor_tensor(cs[:], co_s[:], sc_s[:], ALU.mult).then_inc(cs_ready, 1)
            dve.wait_ge(cs_ready, 1)

            def scale_b(n):
                c, cols = pieces[n]
                dve.wait_ge(b_in[n], 16)
                nc.vector.tensor_scalar(b_s[c][:, cols], b_s[c][:, cols], cs[:, c:c + 1], None,
                                        ALU.mult).then_inc(bsc_ready, 1)

            def split_b(n):
                c, cols = pieces[n]
                dve.wait_ge(bhi_ready, n + 1)
                nc.vector.tensor_tensor(b_lo[:, c, cols], b_s[c][:, cols], fp32(b_hi[:, c, cols]),
                                        ALU.subtract).then_inc(blo_ready, 1)

            def split_a(i, j):
                dc = 2 * i + j
                dve.wait_ge(ahi_ready, dc + 1)
                wait(dve, item_mm[1], dc - 1)
                nc.vector.tensor_tensor(a_lo[j][:], a_s[j][:], fp32(a_hi[j][:]), ALU.subtract).then_inc(alo_ready, 1)

            def add(i, j, half):
                dc = 2 * i + j
                dve.wait_ge(item_mm[half], dc + 1)
                dve.wait_ge(wt_in[j][half], 16 * i + 16)
                nc.vector.tensor_tensor(wt_s[j][half], acc[j][half], wt_s[j][half],
                                        ALU.add).then_inc(item_sum[half], 1)

            def split_w(i, j):
                dc = 2 * i + j
                dve.wait_ge(whi_ready, dc + 1)
                here = (slice(None), bass.ds(dc, 1), slice(None))
                nc.vector.tensor_tensor(w_lo[here].rearrange("p a n -> p (a n)"), wt_s[j][0],
                                        fp32(w_hi[here].rearrange("p a n -> p (a n)")),
                                        ALU.subtract).then_inc(wlo_ready, 1)

            def chunk(i, j):
                add(i, j, 0)
                add(i, j, 1)
                split_w(i, j)

            split_a(0, 0)
            scale_b(0)
            scale_b(1)
            split_b(0)
            split_b(1)
            scale_b(2)
            scale_b(3)
            split_b(2)
            split_b(3)
            split_a(0, 1)
            chunk(0, 0)
            dve.wait_ge(mlp_in, 5 * 16)
            dve.wait_ge(lg_mm, 1)
            nc.vector.tensor_tensor(logits[:], ps_lg, b2_s[:], ALU.add).then_inc(lg_ready, 1)
            dve.wait_ge(lg_ready, 1)
            nc.vector.reduce_max(peak[:], logits[:], AX.X).then_inc(sm_step, 1)
            dve.wait_ge(sm_step, 1)
            nc.vector.tensor_scalar(logits[:], logits[:], peak[:], None, ALU.subtract).then_inc(peak_ready, 1)
            dve.wait_ge(exp_ready, 1)
            nc.vector.reduce_sum(total[:], expo[:], AX.X).then_inc(sm_step, 1)
            dve.wait_ge(sm_step, 2)
            nc.vector.reciprocal(inverse[:], total[:]).then_inc(sm_step, 1)
            dve.wait_ge(sm_step, 3)
            nc.vector.tensor_scalar(att[:], expo[:], inverse[:], None, ALU.mult).then_inc(att_ready, 1)

            def pair(i):
                split_a(i, 0)
                chunk(i - 1, 1)
                split_a(i, 1)
                chunk(i, 0)

            pair(1)
            dve.wait_ge(sh.const_in, 48)
            aggregate(nc, dve, sh, 0, 0)
            with dve.Fori(2, DC // 2) as i:
                pair(i)
            chunk(DC // 2 - 1, 1)


def layer0_block(nc, sh, w_hi, w_lo, x, weff_d, bias, u_d, x1_d, conv_w, ctx_w, cond_t, fside):
    with ExitStack() as ctx:
        def sb(name, shape, dt=F32):
            return ctx.enter_context(nc.sbuf_tensor(name, shape, dt))

        def sem(name):
            return ctx.enter_context(nc.semaphore(name))

        def per_half(name):
            return [sem(f"{name}_{half}") for half in range(2)]

        u_hi = [sb(f"u_hi{j}", [P, L], F32R) for j in range(2)]
        u_lo = [sb(f"u_lo{j}", [P, L], F32R) for j in range(2)]
        x_s = [sh.x0, sb("x_s1", [P, L])]
        u_s = sh.u_s[:, 0:L]
        x1_s = [sh.x1_s[:, j, :].rearrange("p (s q) -> p s q", s=S) for j in range(2)]
        bias_s = sb("bias_s", [P, HALF])
        kern, agg, ps_u, ps_g = sh.kern, sh.agg, sh.ps_u, sh.ps_g
        u_in_s = [u_s, x_s[1][:]]
        x_in_s = [x_s[0][:, 0:HALF], x_s[0][:, HALF:L]]
        stages = [kern[:, 0:HALF], kern[:, HALF:L], x_s[1][:, 0:HALF], x_s[1][:, HALF:L]]
        CW = G * 3 * P
        ctx_w_s, cond_s, fs_s = kern[:, CW:CW + C], kern[:, CW + C:CW + C + NB], kern[:, CW + C + NB:CW + C + NB + G]
        WIDE = 12

        def stage(dc):
            return dc % 4 if dc < WIDE else dc % 2

        def before(dc):
            return max([c + 1 for c in range(dc) if stage(c) == stage(dc)], default=0)

        bias_in = per_half("bias_in")
        w_in = [sem(f"w_in{j}") for j in range(4)]
        whi_ready, wlo_ready, w_free = sem("whi2_ready"), sem("wlo2_ready"), sem("w_free")
        x_in, agg_step, u_mm, x1_out = sh.x_in, sh.agg_step, sh.u_mm, sh.x1_out
        u_in = [sem(f"u_in{j}") for j in range(2)]
        u_out, u_ready = sem("u_out"), sem("u_ready")
        first_add, first_hi, first_lo = sem("first_add"), sem("first_hi"), sem("first_lo")
        ctx_in, cw_zero, ctx_mm, cbias_ready = sem("ctx_in"), sem("cw_zero"), sem("ctx_mm"), sem("cbias_ready")
        uhi_ready, ulo_ready, gemm = per_half("uhi_ready"), per_half("ulo_ready"), per_half("gemm")
        xb_ready, x1_ready = per_half("xb_ready"), per_half("x1_ready")
        block = ctx.enter_context(nc.Block())
        PAIRS = NB // 2

        @block.sync
        def _(sp):
            def load_bias(half):
                sp.dma_start(bias_s[:], bias.rearrange("(a n) -> a n", a=1)[:, half * HALF:(half + 1) * HALF]
                             .to_broadcast([P, HALF])).then_inc(bias_in[half], 16)

            def load_x(i, j):
                n = 2 * i + j
                wait(sp, xb_ready[0], n - 1)
                wait(sp, u_mm, n - 1)
                sp.dma_start(x_s[j][:], x[n, :, :]).then_inc(x_in[0][j], 16)

            def load_x_again(i, j):
                wait(sp, xb_ready[1], 2 * i + j - 1)
                sp.dma_start(x_in_s[j], x[2 * i + j, :, HALF:L]).then_inc(x_in[1][j], 16)

            def load_u(i, j):
                n = 2 * i + j
                wait(sp, uhi_ready[1], n - 1)
                wait(sp, ulo_ready[1], n - 1)
                sp.dma_start(u_in_s[j], u_d[n, :, :]).then_inc(u_in[j], 16)

            def load_w(dc):
                s = stage(dc)
                wait(sp, whi_ready, before(dc))
                wait(sp, wlo_ready, before(dc))
                sp.dma_start(stages[s], weff_d[dc * P:(dc + 1) * P, :]).then_inc(w_in[s], 16)

            load_x(0, 1)
            load_bias(0)
            with sp.Fori(1, PAIRS) as i:
                for j in range(2):
                    load_x(i, j)
            sp.wait_ge(agg_step, K * NB)
            sp.wait_ge(sh.weff_out[0], 16 * (DC // 2))
            sp.wait_ge(sh.weff_out[1], 16 * (DC // 2))
            load_w(0)
            load_w(1)
            sp.wait_ge(u_mm, NB - 1)
            sp.wait_ge(xb_ready[0], NB - 1)
            load_x_again(0, 0)
            sp.wait_ge(u_mm, NB)
            sp.wait_ge(xb_ready[0], NB)
            sp.wait_ge(uhi_ready[0], NB)
            sp.wait_ge(ulo_ready[0], NB)
            sp.wait_ge(u_out, 16 * NB)
            load_u(0, 0)
            load_bias(1)
            for dc in range(2, DC):
                load_w(dc)
                if dc == WIDE + 1:
                    sp.wait_ge(whi_ready, WIDE)
                    sp.wait_ge(wlo_ready, WIDE)
                    load_u(0, 1)
                    load_x_again(0, 1)
            with sp.Fori(1, PAIRS) as i:
                for j in range(2):
                    load_u(i, j)
                    load_x_again(i, j)
            sp.wait_ge(uhi_ready[1], NB - 1)
            sp.wait_ge(ulo_ready[1], NB - 1)
            sp.wait_ge(x1_out[0][0], 16 * PAIRS)
            sp.wait_ge(x1_out[1][0], 16)
            for g in range(2):
                sh.load_group(sp, x1_d, sh.xp[g], g, 0, g)

        @block.gpsimd
        def _(pool):
            def residual(half, i, j):
                n = 2 * i + j
                pool.wait_ge(x_in[half][j], 16 * i + 16)
                wait(pool, x1_out[half][j], 16 * i)
                src = x_s[j][:, 0:HALF] if half == 0 else x_in_s[j]
                nc.gpsimd.tensor_tensor(x1_s[j].rearrange("p s q -> p q s"),
                                        src.rearrange("p (q s) -> p q s", s=S),
                                        bias_s[:].rearrange("p (q s) -> p q s", s=S), ALU.add).then_inc(xb_ready[half], 1)

            def prepare_layer1():
                pool.wait_ge(wlo_ready, DC)
                nc.gpsimd.memset(kern[:, 0:CW], 0.0).then_inc(cw_zero, 1)
                pool.dma_start(ctx_w_s, ctx_w).then_inc(ctx_in, 16)
                pool.dma_start(cond_s, cond_t).then_inc(ctx_in, 16)
                for r in range(S):
                    pool.dma_start(fs_s[r * GC:(r + 1) * GC, :], fside).then_inc(ctx_in, 16)
                pool.wait_ge(cw_zero, 1)
                for s in range(S):
                    for tau in (-1, 0, 1):
                        lo, hi = max(0, 4 * tau + s - 4), min(S - 1, 4 * tau + s + 4)
                        kr = 4 - 4 * tau - s + lo
                        n = hi - lo + 1
                        dst = kern[s * GC:(s + 1) * GC, 0:CW].rearrange("p (g m) -> p g m", g=G)
                        off = (tau + 1) * P + lo * GC
                        pool.dma_start(dst[:, :, off:off + n * GC],
                                       conv_w[:, :, kr * GC:(kr + n) * GC]).then_inc(sh.cw_in, 16)

            pool.wait_ge(sh.weff_out[1], 16 * (DC // 2))
            for half in range(2):
                pool.wait_ge(bias_in[half], 16)
                for j in range(2):
                    if half == 1:
                        pool.wait_ge(x1_out[0][j], 16 * PAIRS)
                    residual(half, 0, j)
                if half == 1:
                    prepare_layer1()
                with pool.Fori(1, PAIRS) as i:
                    residual(half, i, 0)
                    residual(half, i, 1)
            pool.wait_ge(uhi_ready[1], NB - 1)
            pool.wait_ge(ulo_ready[1], NB - 1)
            nc.gpsimd.memset(sh.u_s[:, 0:1], 0.0).then_inc(sh.pad_ready, 1)
            nc.gpsimd.memset(sh.u_s[:, Q + 1:Q + 3], 0.0).then_inc(sh.pad_ready, 1)
            nc.gpsimd.memset(sh.u_s[:, 2 * Q + 3:2 * Q + 4], 0.0).then_inc(sh.pad_ready, 1)

        @block.tensor
        def _(pe):
            def make_u(i, j):
                n = 2 * i + j
                pe.wait_ge(x_in[0][j], 16 * i + 16)
                pe.wait_ge(agg_step, K * (n + 1))
                wait(pe, u_ready, n)
                u_product(nc, sh, x_s[j], j)

            def products(half, i, j, following=None, opening=False, closing=False):
                n = 2 * i + j
                first = half == 0 and isinstance(n, int) and n == 0
                if first:
                    pe.wait_ge(first_lo, 1)
                else:
                    pe.wait_ge(uhi_ready[half], n + 1)
                    pe.wait_ge(ulo_ready[half], n + 1)
                wait(pe, x1_ready[half], n - 1)
                if half == 1 and isinstance(n, int) and n < 2:
                    pe.wait_ge(x1_ready[0], NB - 1 + n)
                for dc in range(DC):
                    if first and dc == DC // 2:
                        pe.wait_ge(ulo_ready[0], 1)
                    if opening:
                        pe.wait_ge(whi_ready, dc + 1)
                        pe.wait_ge(wlo_ready, dc + 1)
                    for u, w in ((u_hi, w_hi), (u_hi, w_lo), (u_lo, w_hi)):
                        for c in range(2):
                            mm = nc.tensor.matmul(ps_g[:, j, c * 512:(c + 1) * 512], u[j][:, dc * P:(dc + 1) * P],
                                                  w[:, dc, c * 512:(c + 1) * 512],
                                                  start=(dc == 0 and u is u_hi and w is w_hi),
                                                  stop=(dc == DC - 1 and u is u_lo))
                    if closing and dc < DC - 1:
                        mm.then_inc(w_free, 1)
                    if dc == DC // 2 - 1 and following is not None:
                        make_u(*following)
                mm.then_inc(gemm[half], 1)

            products(0, 0, 0, (0, 1))
            products(0, 0, 1, (1, 0))
            with pe.Fori(1, PAIRS - 1) as i:
                products(0, i, 0, (i, 1))
                products(0, i, 1, (i + 1, 0))
            products(0, PAIRS - 1, 0, (PAIRS - 1, 1))
            products(0, PAIRS - 1, 1, closing=True)
            products(1, 0, 0, opening=True)
            products(1, 0, 1)
            pe.wait_ge(ctx_in, 16 * 6)
            pe.wait_ge(u_ready, NB)
            for g in range(G):
                for r in range(S):
                    mm = nc.tensor.matmul(ps_u[r * GC:(r + 1) * GC, 0, g * NB:(g + 1) * NB],
                                          ctx_w_s[:, g * GC:(g + 1) * GC], cond_s, start=True, stop=True)
            mm.then_inc(ctx_mm, 1)
            with pe.Fori(1, PAIRS) as i:
                products(1, i, 0)
                products(1, i, 1)

        def w_replaceable(eng, dc):
            if dc < DC - 1:
                eng.wait_ge(w_free, dc + 1)
            else:
                eng.wait_ge(gemm[0], NB)

        @block.scalar
        def _(act):
            def split_u(half, i, j):
                n = 2 * i + j
                if half == 0:
                    act.wait_ge(u_ready, n + 1)
                    act.dma_start(u_d[n, :, :], u_s).then_inc(u_out, 16)
                else:
                    act.wait_ge(u_in[j], 16 * i + 16)
                    if isinstance(n, int) and n < 2:
                        act.wait_ge(gemm[0], NB - 1 + n)
                wait(act, gemm[half], n - 1)
                nc.scalar.activation(u_hi[j][:], u_s if half == 0 else u_in_s[j], ACT.Copy).then_inc(uhi_ready[half], 1)

            def store(half, i, j):
                n = 2 * i + j
                act.wait_ge(x1_ready[half], n + 1)
                act.dma_start(x1_d[n, :, :, half * HALF // S:(half + 1) * HALF // S],
                              x1_s[j]).then_inc(x1_out[half][j], 16)

            act.wait_ge(first_add, 1)
            nc.scalar.activation(u_hi[0][:, 0:HALF], u_s[:, 0:HALF], ACT.Copy).then_inc(first_hi, 1)
            act.wait_ge(u_ready, 1)
            nc.scalar.activation(u_hi[0][:, HALF:L], u_s[:, HALF:L], ACT.Copy).then_inc(uhi_ready[0], 1)
            act.dma_start(u_d[0, :, :], u_s).then_inc(u_out, 16)
            split_u(0, 0, 1)
            store(0, 0, 0)
            with act.Fori(1, PAIRS) as i:
                split_u(0, i, 0)
                store(0, i - 1, 1)
                split_u(0, i, 1)
                store(0, i, 0)
            split_u(1, 0, 0)
            for dc in range(DC):
                s = stage(dc)
                act.wait_ge(w_in[s], 16 * sum(1 for c in range(dc + 1) if stage(c) == s))
                w_replaceable(act, dc)
                nc.scalar.activation(w_hi[:, dc, :], stages[s], ACT.Copy).then_inc(whi_ready, 1)
            split_u(1, 0, 1)
            store(0, PAIRS - 1, 1)
            store(1, 0, 0)
            with act.Fori(1, PAIRS) as i:
                split_u(1, i, 0)
                store(1, i - 1, 1)
                split_u(1, i, 1)
                store(1, i, 0)
            store(1, PAIRS - 1, 1)

        @block.vector
        def _(dve):
            def take_u(half, i, j):
                n = 2 * i + j
                if half == 0:
                    dve.wait_ge(u_mm, n + 1)
                    dve.wait_ge(agg_step, K * (n + 1))
                    wait(dve, uhi_ready[0], n)
                    wait(dve, ulo_ready[0], n)
                    wait(dve, u_out, 16 * n)
                    nc.vector.tensor_tensor(u_s.rearrange("p (c o) -> p c o", c=DC), ps_u[:],
                                            agg[j][:, P:2 * P].unsqueeze(1).to_broadcast([P, DC, P]),
                                            ALU.add).then_inc(u_ready, 1)
                dve.wait_ge(uhi_ready[half], n + 1)
                wait(dve, gemm[half], n - 1)
                nc.vector.tensor_tensor(u_lo[j][:], u_s if half == 0 else u_in_s[j], fp32(u_hi[j][:]),
                                        ALU.subtract).then_inc(ulo_ready[half], 1)

            def take_x1(half, i, j):
                n = 2 * i + j
                dve.wait_ge(gemm[half], n + 1)
                dve.wait_ge(xb_ready[half], n + 1)
                x1 = x1_s[j].rearrange("p s q -> p q s")
                nc.vector.tensor_tensor(x1, ps_g[:, j, :].rearrange("p (q s) -> p q s", s=S), x1,
                                        ALU.add).then_inc(x1_ready[half], 1)

            dve.wait_ge(sh.weff_out[0], 16 * (DC // 2))
            for n, ready in enumerate((first_add, u_ready)):
                here = slice(n * DC // 2, (n + 1) * DC // 2)
                nc.vector.tensor_tensor(u_s.rearrange("p (c o) -> p c o", c=DC)[:, here, :], ps_u[:, here, :],
                                        agg[0][:, P:2 * P].unsqueeze(1).to_broadcast([P, DC // 2, P]),
                                        ALU.add).then_inc(ready, 1)
            for n, (hi_sem, lo_sem) in enumerate(((first_hi, first_lo), (uhi_ready[0], ulo_ready[0]))):
                here = slice(n * HALF, (n + 1) * HALF)
                dve.wait_ge(hi_sem, 1)
                nc.vector.tensor_tensor(u_lo[0][:, here], u_s[:, here], fp32(u_hi[0][:, here]),
                                        ALU.subtract).then_inc(lo_sem, 1)
            aggregate(nc, dve, sh, 1, 1)
            take_u(0, 0, 1)
            aggregate(nc, dve, sh, 2, 0)
            take_x1(0, 0, 0)
            with dve.Fori(1, PAIRS - 1) as i:
                take_u(0, i, 0)
                aggregate(nc, dve, sh, 2 * i + 1, 1)
                take_x1(0, i - 1, 1)
                take_u(0, i, 1)
                aggregate(nc, dve, sh, 2 * i + 2, 0)
                take_x1(0, i, 0)
            take_u(0, PAIRS - 1, 0)
            aggregate(nc, dve, sh, NB - 1, 1)
            take_x1(0, PAIRS - 2, 1)
            take_u(0, PAIRS - 1, 1)
            take_x1(0, PAIRS - 1, 0)
            take_u(1, 0, 0)
            for dc in range(DC):
                dve.wait_ge(whi_ready, dc + 1)
                w_replaceable(dve, dc)
                nc.vector.tensor_tensor(w_lo[:, dc, :], stages[stage(dc)], fp32(w_hi[:, dc, :]),
                                        ALU.subtract).then_inc(wlo_ready, 1)
            take_u(1, 0, 1)
            take_x1(0, PAIRS - 1, 1)
            take_x1(1, 0, 0)
            with dve.Fori(1, PAIRS) as i:
                take_u(1, i, 0)
                take_x1(1, i - 1, 1)
                take_u(1, i, 1)
                take_x1(1, i, 0)
            dve.wait_ge(ctx_mm, 1)
            nc.vector.tensor_tensor(sh.cbias[:], ps_u[:, 0, 0:G * NB].rearrange("p (g b) -> p g b", g=G),
                                    fs_s.unsqueeze(2).to_broadcast([P, G, NB]), ALU.add).then_inc(cbias_ready, 1)
            take_x1(1, PAIRS - 1, 1)


def layer1_block(nc, sh, x1_d, up, down, perm, ident, z_d, y_d, out):
    with ExitStack() as ctx:
        def sb(name, shape, dt=F32):
            return ctx.enter_context(nc.sbuf_tensor(name, shape, dt))

        def sem(name):
            return ctx.enter_context(nc.semaphore(name))

        def bank(name, n=1):
            return ctx.enter_context(nc.psum_tensor(name, [P, n, 512], F32))

        up_hi, up_lo = sb("up_hi", [P, H, M], F32R), sb("up_lo", [P, H, M], F32R)
        dn_hi, dn_lo = sb("dn_hi", [P, H, MC * P], F32R), sb("dn_lo", [P, H, MC * P], F32R)
        cw_hi, cw_lo = sb("cw_hi", [P, G * 3, P], F32R), sb("cw_lo", [P, G * 3, P], F32R)
        xp_hi, xp_lo = sb("xp_hi", [P, Q + 2], F32R), sb("xp_lo", [P, Q + 2], F32R)
        z_s = sb("z_s", [P, Q])
        t_hi, t_lo = sb("t_hi", [P, RB], F32R), sb("t_lo", [P, RB], F32R)
        g_hi, g_lo = sb("g_hi", [P, MC, RB], F32R), sb("g_lo", [P, MC, RB], F32R)
        y_s = [sb(f"y_s{j}", [P, RB]) for j in range(2)]
        rear = sb("rear", [P, 4, 4 * P])
        yt_s = [rear[:, j, :].rearrange("p (l r) -> p l r", l=4) for j in range(2)]
        x1_s = [rear[:, 2 + j, :].rearrange("p (s q) -> p s q", s=S) for j in range(2)]
        results = sb("results", [P, 2, 512])
        o_s = [results[:, j, :] for j in range(2)]
        idx = sb("idx", [P, H], I32)
        id_s = sb("id_s", [P, P])
        xp, t_s, cbias = sh.xp + [results[:].rearrange("p a n -> p (a n)")[:, 0:Q + 2]], sh.t_s, sh.cbias
        g_s = sh.kern[:].rearrange("p (c n) -> p c n", c=MC)
        zt_pair = [sh.x1_s[:].rearrange("p a (w s c) -> p (a w) s c", w=2, s=S),
                   rear[:].rearrange("p w (s c) -> p w s c", s=S)]

        ps_up = bank("ps_up", MC)
        ps_c, ps_zt, ps_y, ps_f = bank("ps_c"), bank("ps_zt"), bank("ps_y"), bank("ps_f")

        small_in, w_in = sem("small_in"), [sem(f"l1w_in{j}") for j in range(4)]
        wsplit_hi, wsplit_lo = sem("wsplit_hi"), sem("wsplit_lo")
        xp_in = sh.xp_in
        xhi_ready, xlo_ready, conv_done, z_ready, zt_done, zt_ready = (sem(n) for n in (
            "xhi_ready", "xlo_ready", "conv_done", "z_ready", "zt_done", "zt_ready"))
        z_out = [sem(f"z_out{j}") for j in range(2)]
        t_in = [sem(f"t_in{j}") for j in range(2)]
        thi_ready, tlo_ready, up_done, gelu_done, ghi_ready, glo_ready, down_done, y_ready = (sem(n) for n in (
            "thi_ready", "tlo_ready", "up_done", "gelu_done", "ghi_ready", "glo_ready", "down_done", "y_ready"))
        ghi_scalar = sem("ghi_scalar")
        gather_clear, scatter_clear = sem("gather_clear"), sem("scatter_clear")
        block_scattered, block_gathered = sem("block_scattered"), sem("block_gathered")
        y_out = [sem(f"y_out{j}") for j in range(2)]
        yt_in = [sem(f"yt_in{j}") for j in range(2)]
        x1_in = [sem(f"x1f_in{j}") for j in range(2)]
        fin_done, o_ready = sem("fin_done"), sem("o_ready")
        o_out = [sem(f"o_out{j}") for j in range(2)]
        last_x1_in = [sem(f"last_x1_in{v}") for v in range(H)]
        last_yt_in, last_o_out = [sem(f"last_yt_in{j}") for j in range(4)], [sem(f"last_o_out{j}") for j in range(4)]
        last_fin, last_o = sem("last_fin"), sem("last_o")
        block = ctx.enter_context(nc.Block())

        STEPS = BLOCKS * H
        stage = [sh.kern[:, j * M:(j + 1) * M] for j in range(4)]
        cw_stage = sh.kern[:, 0:G * 3 * P]
        xp_pair = [(xp_hi[:], xp_lo[:]), (g_hi[:].rearrange("p c n -> p (c n)")[:, 0:Q + 2],
                                          g_lo[:].rearrange("p c n -> p (c n)")[:, 0:Q + 2])]
        ps_conv = [ps_c[:, 0, :], ps_up[:, 0, :]]
        z_pair = [z_s[:], y_s[0][:]]
        chunks = []
        for h in range(H):
            chunks.append((up_hi[:, h, :], up_lo[:, h, :], up[:, h, :]))
            chunks.append((dn_hi[:, h, :], dn_lo[:, h, :], down[:, h, :]))

        def exists(k, h, offset):
            return not isinstance(k, int) or 0 <= H * k + h + offset < STEPS

        def final_exists(k, h, n):
            return not isinstance(k, int) or 0 <= H * (k - 1) + h - n < STEPS - H

        def drive(eng, step):
            for h in range(2 * H - LEAD, H):
                step(-2, h, 0)
            for k in (-1, 0, 1):
                for h in range(H):
                    step(k, h, k % 2)
            with eng.Fori(1, BLOCKS // 2 - 1) as i:
                for parity in range(2):
                    for h in range(H):
                        step(2 * i + parity, h, parity)
            for k in (BLOCKS - 2, BLOCKS - 1):
                for h in range(H):
                    step(k, h, k % 2)
            step(BLOCKS, 0, 0)
            step(BLOCKS, 1, 0)

        left = ([sh.x1_s[:].rearrange("p a n -> p (a n)")[:, n * 512:(n + 1) * 512] for n in range(4)]
                + [xp[j][:, 0:512] for j in range(2)] + [z_s[:]])
        last_x1 = left + [g_s[:, mc, :] for mc in range(MC)]
        ROOMS = len(last_x1)
        last_x1 = (last_x1 + last_x1)[:H]
        last_x1 = [room.rearrange("p (s q) -> p s q", s=S) for room in last_x1]
        last_yt = yt_s + [t.rearrange("p (l r) -> p l r", l=4) for t in t_s]
        last_sum = o_s + [x1.rearrange("p s q -> p (s q)") for x1 in x1_s]
        last_ps = [ps_f[:, 0, :], ps_c[:, 0, :]]

        def last_unit(v):
            return NB - SB + v // 4, v % 4

        def lead(k):
            return isinstance(k, int) and k < 0

        def chunks_of(k, h):
            n = 2 * (H * k + h + LEAD)
            return range(n, min(n + 2, len(chunks)))

        def pair_of(k, h):
            return h % 2 if isinstance(k, int) and k < 0 else 0

        def paired(k, h):
            return isinstance(k, int) and (k < 0 or (k == 0 and h == 0))

        def t_pair(k, h):
            if late(k, h) and h % 2 == 1:
                return xp_hi[:, 0:RB], xp_lo[:, 0:RB]
            return t_hi[:], t_lo[:]

        def xp_of(k, h):
            u = H * k + h + LEAD
            return u % 4 if isinstance(u, int) and u < H else h % 2

        def xp_loads(k, h):
            u = H * k + h + LEAD
            if isinstance(u, int) and u < H:
                return u // 4 + 1
            return H // 2 * k + (h + LEAD) // 2 + 1 - H // 4

        def zt_of(k, h):
            u = H * k + h + LEAD
            return zt_pair[u // G % 2 if isinstance(u, int) and u < H else 0]

        def late(k, h):
            return isinstance(k, int) and H * k + h > STEPS - LEAD

        def early(k, h):
            return isinstance(k, int) and H * k + h > STEPS - LEAD + 1

        def by_scalar(k, h, mc):
            return late(k, h) and mc % 2 == 1

        def scalar_copies(k, h, mc):
            return 2 * (H * k + h - (STEPS - LEAD + 1)) + mc // 2 + 1

        def t_users(k, h):
            s = H * k + h
            return MC * (s - 1 if late(k, h) else s)

        def conv_unit(k, h):
            return H * k + h + LEAD, h % 2, SB * k + (h + LEAD) // G, h % G

        def final_unit(k, h):
            return H * (k - 1) + h, h % 2, SB * (k - 1) + h // 4, h % 4

        def before(k, h, n=1):
            return (k, h - n) if h >= n else (k - 1, h - n + H)

        def after(k, h):
            return (k, h + 1) if h < H - 1 else (k + 1, 0)

        @block.sync
        def _(sp):
            sp.dma_start(id_s[:], ident).then_inc(small_in, 16)
            sp.dma_start(idx[:], perm).then_inc(small_in, 16)

            def load_x1(k, h):
                u, _, b, g = conv_unit(k, h)
                wait(sp, xlo_ready, u - 3 if isinstance(u, int) and u < H + 2 else u - 1)
                j = xp_of(k, h)
                sh.load_group(sp, x1_d, xp[j], j, b, g)

            def load_final(k, h, parity):
                v, j, b, c = final_unit(k, h)
                if h == 0:
                    scattered = 16 * (H // 2) * k
                    if not isinstance(k, int):
                        scattered = sp.snap(scattered)
                    wait(sp, y_out[0], scattered)
                    wait(sp, y_out[1], scattered)
                    sp.sem_inc(block_scattered, 1)
                if isinstance(k, int) and v == 0:
                    sp.wait_ge(z_out[1], 64 * 2)
                wait(sp, fin_done, v - 1)
                sp.dma_start(yt_s[j], y_d[1 - parity][c * 512:(c + 1) * 512, h // 4 * C:(h // 4 + 1) * C]
                             .rearrange("(l p) r -> p l r", p=P)).then_inc(yt_in[j], 16)
                wait(sp, o_ready, v - 1)
                sp.dma_start(x1_s[j], x1_d[b, :, :, c * P:(c + 1) * P]).then_inc(x1_in[j], 16)

            def load_last_x1(v):
                b, c = last_unit(v)
                if v == 0:
                    for j in range(2):
                        sp.wait_ge(z_out[j], 64 * (NB // 2))
                elif v == 4:
                    sp.wait_ge(xlo_ready, STEPS)
                    sp.wait_ge(zt_done, STEPS)
                sp.dma_start(last_x1[v], x1_d[b, :, :, c * P:(c + 1) * P]).then_inc(last_x1_in[v], 16)

            def finish():
                for j in range(2):
                    sp.wait_ge(y_out[j], 16 * (STEPS // 2))
                sp.wait_ge(tlo_ready, STEPS)
                for v in range(H):
                    b, c = last_unit(v)
                    if v < 2:
                        sp.wait_ge(fin_done, STEPS - H - 1 + v)
                    wait(sp, last_fin, v - 3)
                    sp.dma_start(last_yt[v % 4], y_d[(BLOCKS - 1) % 2][c * 512:(c + 1) * 512, v // 4 * C:(v // 4 + 1) * C]
                                 .rearrange("(l p) r -> p l r", p=P)).then_inc(last_yt_in[v % 4], 16)

            def store_out(k, h):
                v, j, b, c = final_unit(k, h)
                sp.wait_ge(o_ready, v + 1)
                sp.dma_start(out[b, :, c * 512:(c + 1) * 512], o_s[j]).then_inc(o_out[j], 16)

            def store_z(k, h, parity):
                u = conv_unit(k, h)[0] - 2
                jb = (h + LEAD - 2) // G % SB
                ahead = (h + LEAD - 2) // G // SB
                if jb == 0:
                    wait(sp, tlo_ready, H * (k + ahead - 1))
                    sp.sem_inc(block_gathered, 1)
                sp.wait_ge(zt_ready, u + 1)
                for w in range(4):
                    sp.dma_start(z_d[(parity + ahead) % 2][w * 512:(w + 1) * 512, jb * C:(jb + 1) * C]
                                 .rearrange("(q r) n -> q r n", r=S), zt_of(*before(k, h, 2))[:, w, :, :]).then_inc(z_out[jb % 2], 16)

            def step(k, h, parity):
                u = H * k + h + LEAD
                if lead(k) and u < H - 2:
                    load_x1(*after(*after(*after(*after(k, h)))))
                elif lead(k) and u >= H:
                    load_x1(*after(*after(k, h)))
                if exists(k, h, LEAD - 2) and (h + LEAD - 2) % G == G - 1:
                    store_z(k, h, parity)
                if not lead(k) and exists(k, h, LEAD + 2):
                    load_x1(*after(*after(k, h)))
                if isinstance(k, int) and k == BLOCKS - 1 and h < len(left):
                    load_last_x1(h)
                if final_exists(k, h, 0):
                    load_final(k, h, parity)
                if final_exists(k, h, 2):
                    store_out(*before(k, h, 2))

            sp.wait_ge(sh.pad_ready, 7)
            load_x1(-2, 2 * H - LEAD + 2)
            load_x1(-2, 2 * H - LEAD + 3)
            sp.wait_ge(sh.x1_out[1][0], 16 * (NB // 2))
            sp.wait_ge(sh.x1_out[1][1], 16 * (NB // 2))
            drive(sp, step)
            finish()
            sp.wait_ge(o_out[0], 16 * ((STEPS - H) // 2))
            sp.wait_ge(o_out[1], 16 * ((STEPS - H) // 2))

        @block.gpsimd
        def _(pool):
            for j in (2, 3):
                nc.gpsimd.memset(xp[j][:, 0:1], 0.0).then_inc(sh.pad_ready, 1)
                nc.gpsimd.memset(xp[j][:, Q + 1:Q + 2], 0.0).then_inc(sh.pad_ready, 1)

            def gather(k, h, parity):
                s, j = H * k + h, h % 2
                if h == 0:
                    pool.wait_ge(z_out[0], 32 * SB * (k + 1))
                    pool.wait_ge(z_out[1], 32 * SB * (k + 1))
                wait(pool, tlo_ready, s - 1)
                pool.sem_inc(gather_clear, 1)
                nc.gpsimd.indirect_dma_start(
                    out=t_s[j], out_offset=None, in_=z_d[parity],
                    in_offset=bass.IndirectOffsetOnAxis(ap=idx[:, h:h + 1], axis=0)).then_inc(t_in[j], 16)

            def load_weights(n):
                if n < len(chunks):
                    pool.wait_ge(wsplit_lo, G + max(n - 3, 0))
                    pool.dma_start(stage[n % 4], chunks[n][2]).then_inc(w_in[n % 4], 16)

            for n in range(4):
                load_weights(n)

            def step(k, h, parity):
                if isinstance(k, int) and k < 0:
                    for n in range(2):
                        load_weights(2 * (H * k + h + LEAD) + 4 + n)
                if exists(k, h, 2):
                    if isinstance(k, int) and H * k + h == -2:
                        pool.wait_ge(small_in, 32)
                        pool.wait_ge(xlo_ready, H - 1)
                    if h < H - 2:
                        gather(k, h + 2, parity)
                    else:
                        gather(k + 1, h + 2 - H, 1 - parity)
                if exists(k, h, 0):
                    s, j = H * k + h, h % 2
                    pool.wait_ge(y_ready, s + 1)
                    if h == 0:
                        wait(pool, yt_in[0], 16 * (H // 2) * (k - 1))
                        wait(pool, yt_in[1], 16 * (H // 2) * (k - 1))
                    pool.sem_inc(scatter_clear, 1)
                    nc.gpsimd.indirect_dma_start(
                        out=y_d[parity], out_offset=bass.IndirectOffsetOnAxis(ap=idx[:, h:h + 1], axis=0),
                        in_=y_s[j][:], in_offset=None).then_inc(y_out[j], 16)

            drive(pool, step)
            pool.wait_ge(glo_ready, MC * STEPS)
            for v in range(len(left), H):
                b, c = last_unit(v)
                wait(pool, last_o, v - ROOMS + 1)
                pool.dma_start(last_x1[v], x1_d[b, :, :, c * P:(c + 1) * P]).then_inc(last_x1_in[v], 16)
            pool.wait_ge(y_out[0], 16 * (STEPS // 2))
            pool.wait_ge(y_out[1], 16 * (STEPS // 2))

        @block.tensor
        def _(pe):
            def up_part(k, h, mc):
                s = H * k + h
                if mc == 0:
                    pe.wait_ge(tlo_ready, s + 1)
                wait(pe, gelu_done, MC * (s - 1) + mc + 1)
                hi, lo = t_pair(k, h)
                for n, (w, t) in enumerate(((up_hi, hi), (up_hi, lo), (up_lo, hi))):
                    mm = nc.tensor.matmul(ps_up[:, mc, :], w[:, h, mc * P:(mc + 1) * P], t,
                                          start=(n == 0), stop=(n == 2))
                mm.then_inc(up_done, 1)

            def down_part(k, h, mc):
                s = H * k + h
                pe.wait_ge(glo_ready, MC * s + mc + 1)
                if mc == 0:
                    wait(pe, y_ready, s)
                for w, g in ((dn_hi, g_hi), (dn_hi, g_lo), (dn_lo, g_hi)):
                    mm = nc.tensor.matmul(ps_y[:, 0, :], w[:, h, mc * P:(mc + 1) * P], g[:, mc, :],
                                          start=(mc == 0 and w is dn_hi and g is g_hi),
                                          stop=(mc == MC - 1 and w is dn_lo))
                mm.then_inc(down_done, 1)

            def conv(k, h):
                u, j, b, g = conv_unit(k, h)
                if isinstance(k, int) and 0 <= u < G:
                    pe.wait_ge(wsplit_lo, g + 1)
                pe.wait_ge(xlo_ready, u + 1)
                wait(pe, z_ready, u - 1 if paired(k, h) else u)
                hi, lo = xp_pair[pair_of(k, h)]
                acc = ps_conv[pair_of(k, h)]
                for tau in range(3):
                    for n, (w, x) in enumerate(((cw_hi, hi), (cw_hi, lo), (cw_lo, hi))):
                        mm = nc.tensor.matmul(acc, w[:, 3 * g + tau, :], x[:, tau:tau + Q],
                                              start=(tau == 0 and n == 0), stop=(tau == 2 and n == 2))
                mm.then_inc(conv_done, 1)

            def turn_z(k, h):
                u, _, _, _ = conv_unit(k, h)
                z = z_pair[pair_of(k, h)]
                if isinstance(k, int) and u == 0:
                    pe.wait_ge(small_in, 32)
                pe.wait_ge(z_ready, u + 1)
                wait(pe, zt_ready, u)
                for w in range(4):
                    mm = nc.tensor.transpose(ps_zt[:, 0, w * P:(w + 1) * P], z[:, w * P:(w + 1) * P], id_s[:])
                mm.then_inc(zt_done, 1)

            def turn_y(k, h):
                v, j, _, _ = final_unit(k, h)
                pe.wait_ge(yt_in[j], 16 * (H // 2 * (k - 1) + h // 2 + 1))
                wait(pe, o_ready, v)
                for l in range(4):
                    mm = nc.tensor.transpose(ps_f[:, 0, l * P:(l + 1) * P], yt_s[j][:, l, :], id_s[:])
                mm.then_inc(fin_done, 1)

            def step(k, h, parity):
                if exists(k, h, LEAD):
                    conv(k, h)
                if exists(k, h, LEAD - 1):
                    turn_z(*before(k, h))
                if final_exists(k, h, 1):
                    turn_y(*before(k, h))
                if isinstance(k, int) and H * k + h == -1:
                    pe.wait_ge(wsplit_lo, G + len(chunks))
                    pe.wait_ge(z_ready, LEAD)
                for mc in range(MC):
                    if exists(k, h, 0):
                        down_part(k, h, mc)
                    if exists(k, h, 1):
                        up_part(*after(k, h), mc)

            drive(pe, step)
            for v in range(H):
                pe.wait_ge(last_yt_in[v % 4], 16 * (v // 4 + 1))
                if v == 0:
                    pe.wait_ge(o_ready, STEPS - H)
                    pe.wait_ge(z_ready, STEPS)
                wait(pe, last_o, v - 1)
                for l in range(4):
                    mm = nc.tensor.transpose(last_ps[v % 2][:, l * P:(l + 1) * P], last_yt[v % 4][:, l, :], id_s[:])
                mm.then_inc(last_fin, 1)

        @block.scalar
        def _(act):
            def split_kernel(g):
                here = slice(3 * g * P, 3 * (g + 1) * P)
                nc.scalar.activation(cw_hi[:].rearrange("p a b -> p (a b)")[:, here], cw_stage[:, here],
                                     ACT.Copy).then_inc(wsplit_hi, 1)

            def split_weights(n):
                act.wait_ge(w_in[n % 4], 16 * (n // 4 + 1))
                nc.scalar.activation(chunks[n][0], stage[n % 4], ACT.Copy).then_inc(wsplit_hi, 1)

            def split_x(k, h):
                u, j, _, _ = conv_unit(k, h)
                act.wait_ge(xp_in[xp_of(k, h)], 64 * xp_loads(k, h))
                if isinstance(k, int) and u == 2:
                    act.wait_ge(sh.pad_ready, 7)
                wait(act, conv_done, u - 1 if paired(k, h) else u)
                nc.scalar.activation(xp_pair[pair_of(k, h)][0], xp[xp_of(k, h)], ACT.Copy).then_inc(xhi_ready, 1)

            def split_t(k, h):
                s, j = H * k + h, h % 2
                act.wait_ge(t_in[j], 16 * (H // 2 * k + h // 2 + 1))
                wait(act, up_done, t_users(k, h))
                if isinstance(k, int) and s == STEPS - LEAD + 1:
                    act.wait_ge(conv_done, STEPS)
                nc.scalar.activation(t_pair(k, h)[0], t_s[j], ACT.Copy).then_inc(thi_ready, 1)

            act.wait_ge(sh.cw_in, 16 * 12)
            split_kernel(0)
            act.wait_ge(sh.pad_ready, 3)
            split_x(-2, 2 * H - LEAD)
            for g in range(1, G):
                split_kernel(g)

            def gelu(k, h, mc):
                s = H * k + h
                act.wait_ge(up_done, MC * s + mc + 1)
                wait(act, glo_ready, MC * (s - 1) + mc + 1)
                nc.scalar.activation(g_s[:, mc, :], ps_up[:, mc, :], ACT.Gelu).then_inc(gelu_done, 1)
                if by_scalar(k, h, mc):
                    act.wait_ge(gelu_done, MC * s + mc + 1)
                    act.wait_ge(down_done, MC * (s - 1) + mc + 1)
                    nc.scalar.activation(g_hi[:, mc, :], g_s[:, mc, :], ACT.Copy).then_inc(ghi_scalar, 1)

            def step(k, h, parity):
                if not lead(k) and exists(k, h, 1) and not early(*after(k, h)):
                    split_t(*after(k, h))
                if lead(k):
                    split_x(*after(k, h))
                    for n in chunks_of(k, h):
                        split_weights(n)
                if exists(k, h, LEAD):
                    u, j, b, g = conv_unit(k, h)
                    act.wait_ge(conv_done, u + 1)
                    wait(act, zt_done, u - 1 if paired(k, h) else u)
                    nc.scalar.activation(z_pair[pair_of(k, h)], ps_conv[pair_of(k, h)], ACT.Identity,
                                         bias=cbias[:, g, bass.ds(b, 1)]).then_inc(z_ready, 1)
                    if not lead(k) and exists(k, h, LEAD + 1):
                        split_x(*after(k, h))
                if isinstance(k, int) and H * k + h == -1:
                    split_t(0, 0)
                    act.wait_ge(wsplit_lo, G + len(chunks))
                for mc in range(MC - 1):
                    if exists(k, h, 1):
                        gelu(*after(k, h), mc)
                if exists(k, h, 2) and early(*after(*after(k, h))):
                    split_t(*after(*after(k, h)))
                if exists(k, h, 0):
                    s, j = H * k + h, h % 2
                    act.wait_ge(down_done, MC * (s + 1))
                    wait(act, y_out[j], 16 * (H // 2 * k + h // 2))
                    nc.scalar.activation(y_s[j][:], ps_y[:, 0, :], ACT.Copy).then_inc(y_ready, 1)
                if exists(k, h, 1):
                    gelu(*after(k, h), MC - 1)

            drive(act, step)
            for v in range(H):
                b, c = last_unit(v)
                act.wait_ge(last_o, v + 1)
                act.dma_start(out[b, :, c * 512:(c + 1) * 512], last_sum[v % 4]).then_inc(last_o_out[v % 4], 16)
            for j in range(4):
                act.wait_ge(last_o_out[j], 16 * (H // 4))

        @block.vector
        def _(dve):
            def split_kernel(g):
                here = slice(3 * g * P, 3 * (g + 1) * P)
                dve.wait_ge(wsplit_hi, g + 1)
                nc.vector.tensor_tensor(cw_lo[:].rearrange("p a b -> p (a b)")[:, here], cw_stage[:, here],
                                        fp32(cw_hi[:].rearrange("p a b -> p (a b)")[:, here]),
                                        ALU.subtract).then_inc(wsplit_lo, 1)

            def split_weights(n):
                hi, lo, _ = chunks[n]
                dve.wait_ge(wsplit_hi, G + n + 1)
                nc.vector.tensor_tensor(lo, stage[n % 4], fp32(hi),
                                        ALU.subtract).then_inc(wsplit_lo, 1)

            def split_x(k, h):
                u, j, _, _ = conv_unit(k, h)
                dve.wait_ge(xhi_ready, u + 1)
                wait(dve, conv_done, u - 1 if paired(k, h) else u)
                hi, lo = xp_pair[pair_of(k, h)]
                nc.vector.tensor_tensor(lo, xp[xp_of(k, h)], fp32(hi), ALU.subtract).then_inc(xlo_ready, 1)

            def split_t(k, h):
                s, j = H * k + h, h % 2
                dve.wait_ge(thi_ready, s + 1)
                wait(dve, up_done, t_users(k, h))
                if isinstance(k, int) and s == STEPS - LEAD + 1:
                    dve.wait_ge(conv_done, STEPS)
                hi, lo = t_pair(k, h)
                nc.vector.tensor_tensor(lo, t_s[j], fp32(hi), ALU.subtract).then_inc(tlo_ready, 1)

            def take_z(k, h):
                u, j, b, g = conv_unit(k, h)
                dve.wait_ge(zt_done, u + 1)
                if isinstance(k, int) and u == 0:
                    dve.wait_ge(sh.x1_out[1][0], 16 * (NB // 2))
                    dve.wait_ge(sh.x1_out[1][1], 16 * (NB // 2))
                if g == 0:
                    q = (h + LEAD) // G
                    if isinstance(b, int) and b <= SB:
                        wait(dve, z_out[q % 2], 64 * (b // 2))
                    else:
                        wait(dve, z_out[(q + 1) % 2], 64 * (SB // 2 * k + (q + 1) // 2))
                nc.vector.tensor_copy(zt_of(k, h)[:, :, :, g * GC:(g + 1) * GC],
                                      ps_zt[:, 0, :].rearrange("p (w r o) -> p w r o", w=4, r=S)).then_inc(zt_ready, 1)

            def take_final(k, h):
                v, j, b, c = final_unit(k, h)
                n = H // 2 * (k - 1) + h // 2
                dve.wait_ge(fin_done, v + 1)
                dve.wait_ge(x1_in[j], 16 * (n + 1))
                wait(dve, o_out[j], 16 * n)
                nc.vector.tensor_tensor(o_s[j].rearrange("p (q s) -> p q s", s=S),
                                        ps_f[:, 0, :].rearrange("p (q s) -> p q s", s=S),
                                        x1_s[j].rearrange("p s q -> p q s"), ALU.add).then_inc(o_ready, 1)

            split_kernel(0)
            split_x(-2, 2 * H - LEAD)
            for g in range(1, G):
                split_kernel(g)

            def split_g(k, h, mc):
                s = H * k + h
                dve.wait_ge(gelu_done, MC * s + mc + 1)
                wait(dve, down_done, MC * (s - 1) + mc + 1)
                if by_scalar(k, h, mc):
                    dve.wait_ge(ghi_scalar, scalar_copies(k, h, mc))
                else:
                    nc.vector.tensor_copy(g_hi[:, mc, :], g_s[:, mc, :]).then_inc(ghi_ready, 1)
                    n = MC * s + mc + 1
                    if late(k, h):
                        n -= scalar_copies(k, h, mc) - (mc // 2 + 1) + (mc + 1) // 2
                    dve.wait_ge(ghi_ready, n)
                nc.vector.tensor_tensor(g_lo[:, mc, :], g_s[:, mc, :], fp32(g_hi[:, mc, :]),
                                        ALU.subtract).then_inc(glo_ready, 1)

            def step(k, h, parity):
                if not lead(k) and exists(k, h, 1) and not early(*after(k, h)):
                    split_t(*after(k, h))
                if lead(k):
                    split_x(*after(k, h))
                    for n in chunks_of(k, h):
                        split_weights(n)
                if exists(k, h, LEAD - 1):
                    take_z(*before(k, h))
                if final_exists(k, h, 1):
                    take_final(*before(k, h))
                if not lead(k) and exists(k, h, LEAD + 1):
                    split_x(*after(k, h))
                if isinstance(k, int) and H * k + h == -1:
                    split_t(0, 0)
                if exists(k, h, 1):
                    for mc in range(MC):
                        split_g(*after(k, h), mc)
                        if mc == MC - 2 and exists(k, h, 2) and early(*after(*after(k, h))):
                            split_t(*after(*after(k, h)))

            drive(dve, step)
            dve.wait_ge(o_ready, STEPS - H)
            for v in range(H):
                dve.wait_ge(last_fin, v + 1)
                dve.wait_ge(last_x1_in[v], 16)
                if v < 2:
                    dve.wait_ge(o_out[v], 16 * ((STEPS - H) // 2))
                wait(dve, last_o_out[v % 4], 16 * (v // 4))
                nc.vector.tensor_tensor(last_sum[v % 4].rearrange("p (q s) -> p q s", s=S),
                                        last_ps[v % 2].rearrange("p (q s) -> p q s", s=S),
                                        last_x1[v].rearrange("p s q -> p q s"), ALU.add).then_inc(last_o, 1)


def build(nc, x, cond_t, fside, w0, b0, w1, b1, w2, b2, cond_w, bias_k, w_t, bias, lora_a, lora_b, coeffs, scales,
          conv_w, ctx_w, up, down, perm, ident, out):
    def scratch(name, shape):
        return nc.dram_tensor(name, shape, F32, kind="Internal").ap()

    att_d = scratch("att_d", [NB, K])
    weff_d = scratch("weff_d", [L, HALF])
    u_d = scratch("u_d", [NB, P, DC * P])
    x1_d = scratch("x1_d", [NB, C, S, Q])
    z_d = [scratch(f"z_d{j}", [L, RB]) for j in range(2)]
    y_d = [scratch(f"y_d{j}", [L, RB]) for j in range(2)]
    with ExitStack() as ctx:
        sh = Shared(nc, ctx)
        with ExitStack() as ctx0:
            sh.add_layer0(nc, ctx0)
            w_hi = ctx0.enter_context(nc.sbuf_tensor("w_hi", [P, DC, HALF], F32R))
            w_lo = ctx0.enter_context(nc.sbuf_tensor("w_lo", [P, DC, HALF], F32R))
            setup_block(nc, sh, w_hi, w_lo, x, cond_w, bias_k, cond_t, w0, b0, w1, b1, w2, b2, w_t, lora_a, lora_b,
                        coeffs, scales, att_d, weff_d)
            layer0_block(nc, sh, w_hi, w_lo, x, weff_d, bias, u_d, x1_d, conv_w, ctx_w, cond_t, fside)
        layer1_block(nc, sh, x1_d, up, down, perm, ident, z_d, y_d, out)


def kernel(**inputs):
    import numpy as np
    import concourse.bacc as bacc
    from concourse.bass_utils import run_bass_kernel_spmd

    def v(name):
        return np.asarray(inputs[name])

    def by_partition(a):
        return a.reshape(KC, P).T

    def repeat_rank(a):
        return np.broadcast_to(a[:, None], (16, 16)).reshape(ER)

    arrays = {
        "x": v("x"),
        "cond_t": v("cond_128").T,
        "fside": v("fside_S_0").reshape(G, GC).T,
        "w0": v("L0_cond_W0"), "b0": v("L0_cond_b0"),
        "w1": v("L0_cond_W1"), "b1": v("L0_cond_b1"),
        "w2": v("L0_cond_W2"), "b2": v("L0_cond_b2"),
        "cond_w": v("L0_cond_weight")[..., 0].transpose(2, 0, 1),
        "bias_k": v("L0_cond_bias_k"),
        "w_t": v("L0_ffn_W").T,
        "bias": v("L0_ffn_bias"),
        "lora_a": v("L0_ffn_A").reshape(ER, L),
        "lora_b": v("L0_ffn_Bf").transpose(0, 2, 1).reshape(ER, L),
        "coeffs": by_partition(repeat_rank(v("L0_ffn_coeffs"))),
        "scales": by_partition(repeat_rank(v("L0_ffn_scales"))),
        "conv_w": v("L1_cond_weight").reshape(G, GC, GC, TAPS)[..., ::-1].transpose(2, 0, 3, 1).reshape(GC, G, TAPS * GC),
        "ctx_w": v("L1_cond_c_weight").T,
        "up": v("L1_ffn_up").transpose(1, 0, 2),
        "down": v("L1_ffn_down").reshape(H, MC, P, P).transpose(2, 0, 1, 3).reshape(P, H, MC * P),
        "perm": v("L1_ffn_perm").reshape(H, P).T,
        "ident": np.eye(P, dtype=np.float32),
    }
    nc = bacc.Bacc("TRN2", target_bir_lowering=False, num_devices=1)
    args, feed = [], {}
    for name, a in arrays.items():
        a = np.ascontiguousarray(a)
        feed[f"in_{name}"] = a
        args.append(nc.dram_tensor(f"in_{name}", a.shape, mybir.dt.from_np(a.dtype), kind="ExternalInput").ap())
    out = nc.dram_tensor("out_0_dram", (NB, C, L), F32, kind="ExternalOutput").ap()
    build(nc, *args, out)
    r = run_bass_kernel_spmd(nc, [feed], core_ids=[0])
    return r.results[0]["out_0_dram"]
```
